# Optimizing a Trainium2 kernel written in Bass

```python
import numpy as np
import jax
import jax.numpy as jnp

def _softmax(x, axis=-1):
    return jax.nn.softmax(x, axis=axis)

def _gelu(x):
    return jax.nn.gelu(x, approximate=True)

def _silu(x):
    return jax.nn.silu(x)

def _sigmoid(x):
    return jax.nn.sigmoid(x)

def _layernorm(x, axis=-1, eps=1e-05):
    m = jnp.mean(x, axis=axis, keepdims=True)
    v = jnp.var(x, axis=axis, keepdims=True)
    return (x - m) / jnp.sqrt(v + eps)

def _scatter_add(tgt, idx, src, axis=0):
    return tgt.at[idx].add(src)

def _segment_sum(src, seg, n):
    return jax.ops.segment_sum(src, seg, n)
kernel_name = 'mk_decoder_preln_d1_seqx_r8_1df686'

def setup_inputs(seed: int=0):
    np.random.seed(seed)
    _w = jnp.asarray

    def _rec_inputs():
        import jax
        import jax.numpy as jnp
        _rk = jax.random.key(seed)
        x = -0.0005207 + 1.001 * jax.random.normal(jax.random.fold_in(_rk, 1), (8, 128, 512), jnp.float32)
        _lenS = 128 - jax.random.randint(jax.random.fold_in(_rk, 7), (8,), 0, max(1, 128 // 4) + 1, jnp.int32)
        _lenS2 = 128 - jax.random.randint(jax.random.fold_in(_rk, 8), (8,), 0, max(1, 128 // 4) + 1, jnp.int32)
        _ctx_4096P = jax.random.normal(jax.random.fold_in(_rk, 11), (8, 16, 512), jnp.float32)
        _ctx_4096c = jax.random.dirichlet(jax.random.fold_in(_rk, 511), 0.3 * jnp.ones((16,), jnp.float32), (8, 128))
        _ctx_4096t = jnp.einsum('bsk,bkd->bsd', _ctx_4096c, _ctx_4096P)
        _ctx_4096t = _ctx_4096t * jax.lax.rsqrt(jnp.mean(jnp.square(_ctx_4096t)) + 1e-12) * 0.953939
        ctx_4096 = -0.00010331 + 0.999899 * (_ctx_4096t + 0.3 * jax.random.normal(jax.random.fold_in(_rk, 611), (8, 128, 512), jnp.float32))
        return (x, ctx_4096)
    x, ctx_4096 = _rec_inputs()

    def _L0_attn_setup():
        import jax, jax.numpy as jnp
        import numpy as np
        H = 32
        HKV = 8
        D = 512
        HD = D // H
        S = 128
        MASK_OUT = 0.9
        MIN_REMAIN = 128
        THETA = 10000.0

        def rope_tables(seq_len, hd):
            inv_freq = 1.0 / THETA ** (jnp.arange(0, hd, 2, dtype=jnp.float32) / hd)
            t = jnp.arange(seq_len, dtype=jnp.float32)
            freqs = jnp.outer(t, inv_freq)
            emb = jnp.concatenate([freqs, freqs], axis=-1)
            return (jnp.cos(emb), jnp.sin(emb))

        def rotate_half(x):
            x1, x2 = jnp.split(x, 2, axis=-1)
            return jnp.concatenate([-x2, x1], axis=-1)

        def apply_rope(x, cos, sin):
            return x * cos + rotate_half(x) * sin
        key = jax.random.key(seed)
        k0, k1, k2, k3, k4 = jax.random.split(key, 5)
        hidden_states = jax.random.normal(k0, (1, S, D), jnp.float32)
        Wq = jax.random.normal(k1, (D, D), jnp.float32) * 0.02
        Wk = jax.random.normal(k2, (HKV * HD, D), jnp.float32) * 0.02
        Wv = jax.random.normal(k3, (HKV * HD, D), jnp.float32) * 0.02
        Wo = jax.random.normal(k4, (D, D), jnp.float32) * 0.02
        return {'hidden_states': hidden_states, 'Wq': Wq, 'Wk': Wk, 'Wv': Wv, 'Wo': Wo}
    _L0_attn_all = _L0_attn_setup()
    _L0_attn_in = {k: v for k, v in _L0_attn_all.items() if k in ('Wq', 'Wk', 'Wv', 'Wo')}
    del _L0_attn_all

    def _L0_xattn_setup():
        import jax, jax.numpy as jnp
        import numpy as np
        HEADS = 32
        KV_HEADS = 8
        HEAD_DIM = 128
        EPS = 1e-06

        def rms_norm(x, w):
            var = jnp.mean(jnp.square(x.astype(jnp.float32)), axis=-1, keepdims=True)
            return (x.astype(jnp.float32) * jax.lax.rsqrt(var + EPS)).astype(x.dtype) * w
        key = jax.random.key(seed)
        ks = jax.random.split(key, 6)
        bsz, n_lat, seq, hidden = (8, 64, 512, 512)
        return {'latents': jax.random.normal(ks[0], (bsz, n_lat, hidden), jnp.float32), 'context': jax.random.normal(ks[1], (bsz, seq, hidden), jnp.float32), 'Wq': jax.random.normal(ks[2], (hidden, HEADS * HEAD_DIM), jnp.float32) * 0.02, 'Wk': jax.random.normal(ks[3], (hidden, KV_HEADS * HEAD_DIM), jnp.float32) * 0.02, 'Wv': jax.random.normal(ks[4], (hidden, KV_HEADS * HEAD_DIM), jnp.float32) * 0.02, 'Wo': jax.random.normal(ks[5], (HEADS * HEAD_DIM, hidden), jnp.float32) * 0.02, 'q_norm_w': jnp.ones((HEAD_DIM,), jnp.float32), 'k_norm_w': jnp.ones((HEAD_DIM,), jnp.float32)}
    _L0_xattn_all = _L0_xattn_setup()
    _L0_xattn_in = {k: v for k, v in _L0_xattn_all.items() if k in ('Wq', 'Wk', 'Wv', 'Wo', 'q_norm_w', 'k_norm_w')}
    del _L0_xattn_all

    def _L0_ffn_setup():
        import jax, jax.numpy as jnp
        import numpy as np
        OUT, IN = (512, 512)
        GROUP = 32
        NUM_GROUPS = OUT * IN // GROUP

        def _dequantize_4bit(weight_q4, weight_scale):
            low = weight_q4 & 15
            high = weight_q4 >> 4 & 15
            q8 = jnp.stack([low, high], axis=-1).reshape(weight_q4.shape[0], -1)
            x_norm = q8.astype(jnp.float32) / 15.0
            return x_norm * (2.0 * weight_scale) - weight_scale
        key = jax.random.key(seed)
        k1, k2, k3, k4 = jax.random.split(key, 4)
        x = jax.random.normal(k1, (4, 256, IN), dtype=jnp.float32)
        weight_q4 = jax.random.randint(k2, (NUM_GROUPS, GROUP // 2), 0, 32, dtype=jnp.int32)
        weight_scale = jax.random.uniform(k3, (NUM_GROUPS, 1), dtype=jnp.float32)
        bias = jax.random.normal(k4, (OUT,), dtype=jnp.float32)
        return {'x': x, 'weight_q4': weight_q4, 'weight_scale': weight_scale, 'bias': bias}
    _L0_ffn_all = _L0_ffn_setup()
    _L0_ffn_in = {k: v for k, v in _L0_ffn_all.items() if k in ('weight_q4', 'weight_scale', 'bias')}
    del _L0_ffn_all
    return {'x': x, 'ctx_4096': ctx_4096, 'L0_attn_Wq': _L0_attn_in['Wq'], 'L0_attn_Wk': _L0_attn_in['Wk'], 'L0_attn_Wv': _L0_attn_in['Wv'], 'L0_attn_Wo': _L0_attn_in['Wo'], 'L0_xattn_Wq': _L0_xattn_in['Wq'], 'L0_xattn_Wk': _L0_xattn_in['Wk'], 'L0_xattn_Wv': _L0_xattn_in['Wv'], 'L0_xattn_Wo': _L0_xattn_in['Wo'], 'L0_xattn_q_norm_w': _L0_xattn_in['q_norm_w'], 'L0_xattn_k_norm_w': _L0_xattn_in['k_norm_w'], 'L0_ffn_weight_q4': _L0_ffn_in['weight_q4'], 'L0_ffn_weight_scale': _L0_ffn_in['weight_scale'], 'L0_ffn_bias': _L0_ffn_in['bias']}

def reference(x, ctx_4096, L0_attn_Wq, L0_attn_Wk, L0_attn_Wv, L0_attn_Wo, L0_xattn_Wq, L0_xattn_Wk, L0_xattn_Wv, L0_xattn_Wo, L0_xattn_q_norm_w, L0_xattn_k_norm_w, L0_ffn_weight_q4, L0_ffn_weight_scale, L0_ffn_bias):
    import jax
    import jax.numpy as jnp

    def _L0_attn_ref(hidden_states, Wq, Wk, Wv, Wo):
        import jax, jax.numpy as jnp
        import numpy as np
        H = 32
        HKV = 8
        D = 512
        HD = D // H
        S = 128
        MASK_OUT = 0.9
        MIN_REMAIN = 128
        THETA = 10000.0

        def rope_tables(seq_len, hd):
            inv_freq = 1.0 / THETA ** (jnp.arange(0, hd, 2, dtype=jnp.float32) / hd)
            t = jnp.arange(seq_len, dtype=jnp.float32)
            freqs = jnp.outer(t, inv_freq)
            emb = jnp.concatenate([freqs, freqs], axis=-1)
            return (jnp.cos(emb), jnp.sin(emb))

        def rotate_half(x):
            x1, x2 = jnp.split(x, 2, axis=-1)
            return jnp.concatenate([-x2, x1], axis=-1)

        def apply_rope(x, cos, sin):
            return x * cos + rotate_half(x) * sin
        B, Sq, Dm = hidden_states.shape
        dtype = hidden_states.dtype
        neg = jnp.finfo(dtype).min
        q = (hidden_states @ Wq.T).reshape(B, Sq, H, HD).transpose(0, 2, 1, 3)
        k = (hidden_states @ Wk.T).reshape(B, Sq, HKV, HD).transpose(0, 2, 1, 3)
        v = (hidden_states @ Wv.T).reshape(B, Sq, HKV, HD).transpose(0, 2, 1, 3)
        rep = H // HKV
        k = jnp.repeat(k, rep, axis=1)
        v = jnp.repeat(v, rep, axis=1)
        cos, sin = rope_tables(Sq, HD)
        qr = apply_rope(q, cos, sin)
        kr = apply_rope(k, cos, sin)
        draft = jnp.einsum('bhqd,bhkd->bhqk', qr, kr)
        qi = jnp.arange(Sq)
        ki = jnp.arange(Sq)
        causal_future = qi[:, None] < ki[None, :]
        draft = draft + jnp.where(causal_future, neg, jnp.asarray(0.0, dtype))
        num_remain = max(min(Sq, MIN_REMAIN), Sq - int(Sq * MASK_OUT))
        _, draft_indices = jax.lax.top_k(draft, num_remain)
        mask = jnp.full((B, H, Sq, Sq), neg, dtype)
        b_idx = jnp.arange(B)[:, None, None, None]
        h_idx = jnp.arange(H)[None, :, None, None]
        s_idx = jnp.arange(Sq)[None, None, :, None]
        mask = mask.at[b_idx, h_idx, s_idx, draft_indices].set(0.0)
        mask = jnp.where(causal_future[None, None, :, :], neg, mask)
        scores = jnp.einsum('bhqd,bhkd->bhqk', qr, kr) / np.sqrt(HD).astype(np.float32) + mask
        attn = jax.nn.softmax(scores, axis=-1)
        out = jnp.einsum('bhqk,bhkd->bhqd', attn, v)
        out = out.transpose(0, 2, 1, 3).reshape(B, Sq, Dm)
        return out @ Wo.T

    def _L0_xattn_ref(latents, context, Wq, Wk, Wv, Wo, q_norm_w, k_norm_w):
        import jax, jax.numpy as jnp
        import numpy as np
        HEADS = 32
        KV_HEADS = 8
        HEAD_DIM = 128
        EPS = 1e-06

        def rms_norm(x, w):
            var = jnp.mean(jnp.square(x.astype(jnp.float32)), axis=-1, keepdims=True)
            return (x.astype(jnp.float32) * jax.lax.rsqrt(var + EPS)).astype(x.dtype) * w
        bsz, q_len, hidden = latents.shape
        kv = jnp.concatenate([context, latents], axis=1)
        kv_len = kv.shape[1]
        groups = HEADS // KV_HEADS
        q = (latents @ Wq).reshape(bsz, q_len, HEADS, HEAD_DIM).transpose(0, 2, 1, 3)
        k = (kv @ Wk).reshape(bsz, kv_len, KV_HEADS, HEAD_DIM).transpose(0, 2, 1, 3)
        v = (kv @ Wv).reshape(bsz, kv_len, KV_HEADS, HEAD_DIM).transpose(0, 2, 1, 3)
        q = rms_norm(q, q_norm_w)
        k = rms_norm(k, k_norm_w)
        qg = q.reshape(bsz, KV_HEADS, groups, q_len, HEAD_DIM)
        scale = 1.0 / np.sqrt(HEAD_DIM)
        scores = jnp.einsum('bhgqd,bhkd->bhgqk', qg, k) * scale
        probs = jax.nn.softmax(scores.astype(jnp.float32), axis=-1).astype(q.dtype)
        out = jnp.einsum('bhgqk,bhkd->bhgqd', probs, v)
        out = out.reshape(bsz, HEADS, q_len, HEAD_DIM).transpose(0, 2, 1, 3)
        out = out.reshape(bsz, q_len, HEADS * HEAD_DIM)
        return out @ Wo

    def _L0_ffn_ref(x, weight_q4, weight_scale, bias):
        import jax, jax.numpy as jnp
        import numpy as np
        OUT, IN = (512, 512)
        GROUP = 32
        NUM_GROUPS = OUT * IN // GROUP

        def _dequantize_4bit(weight_q4, weight_scale):
            low = weight_q4 & 15
            high = weight_q4 >> 4 & 15
            q8 = jnp.stack([low, high], axis=-1).reshape(weight_q4.shape[0], -1)
            x_norm = q8.astype(jnp.float32) / 15.0
            return x_norm * (2.0 * weight_scale) - weight_scale
        w = _dequantize_4bit(weight_q4, weight_scale).reshape(OUT, IN)
        return jnp.einsum('bsi,oi->bso', x, w) + bias
    x = x + _L0_attn_ref(_layernorm(x, axis=-1), L0_attn_Wq, L0_attn_Wk, L0_attn_Wv, L0_attn_Wo)
    x = x + _L0_xattn_ref(_layernorm(x, axis=-1), ctx_4096, L0_xattn_Wq, L0_xattn_Wk, L0_xattn_Wv, L0_xattn_Wo, L0_xattn_q_norm_w, L0_xattn_k_norm_w)
    x = x + _L0_ffn_ref(_layernorm(x, axis=-1), L0_ffn_weight_q4, L0_ffn_weight_scale, L0_ffn_bias)
    return x

_drawn_inputs = setup_inputs


def setup_inputs(seed=0):
    import zlib

    import numpy as np

    out = dict(_drawn_inputs(seed))
    spreads = {'L0_xattn_q_norm_w': (1.0, 0.6), 'L0_xattn_k_norm_w': (1.0, 0.6)}
    factors = {'L0_attn_Wq': 6.914, 'L0_attn_Wk': 6.078}
    for name, (base, spread) in spreads.items():
        noise = np.random.default_rng([zlib.crc32(name.encode()), seed]).standard_normal(out[name].shape)
        drawn = base * np.exp(spread * noise) if base else spread * noise
        out[name] = jnp.asarray(drawn.astype(out[name].dtype))
    for name, factor in factors.items():
        out[name] = (out[name] * factor).astype(out[name].dtype)
    return out
```

```python
from contextlib import ExitStack

import concourse.bass as bass
from concourse import mybir

ALU = mybir.AluOpType
ACT = mybir.ActivationFunctionType
AX = mybir.AxisListType
F32 = mybir.dt.float32
F32R = mybir.dt.float32r
BF16 = mybir.dt.bfloat16
I32 = mybir.dt.int32

P = 128
B, S, D = 8, 128, 512
C = D // P
H, KVH, HD = 32, 8, 16
G = H // KVH
HALF = HD // 2
XKVH, XG, XD = 8, 4, 128
KV = 2 * S
LN_EPS, RMS_EPS = 1e-5, 1e-6
NEG = -3.3895313892515355e38
STACK = 4 * HD


def wait(eng, sem, count):
    if not (isinstance(count, int) and count <= 0):
        eng.wait_ge(sem, count)


def wait_apart(eng, sem, count, started):
    if not isinstance(count, int):
        count = eng.snap(count)
    eng.wait_ge(started, 1)
    wait(eng, sem, count)


def f32(ap):
    return ap.bitcast(F32)


def steps(eng, count, body):
    body(0, True, False)
    with eng.Fori(1, count - 1) as step:
        body(step, False, False)
    body(count - 1, False, True)


def split_matmuls(pe, out, parts, start=True, stop=True):
    terms = [(a, b) for lh, ll, rh, rl in parts for a, b in ((lh, rh), (lh, rl), (ll, rh))]
    for i, (lhsT, rhs) in enumerate(terms):
        mm = pe.matmul(out, lhsT, rhs, start=start and i == 0, stop=stop and i == len(terms) - 1)
    return mm


def self_attention(nc, mem, io):
    with ExitStack() as ctx:
        def sb(name, shape, dt=F32):
            return ctx.enter_context(nc.sbuf_tensor(name, shape, dt))

        def ps(name, shape=(P, 512)):
            return ctx.enter_context(nc.psum_tensor(name, list(shape), F32))

        def signals(names):
            return [ctx.enter_context(nc.semaphore(name)) for name in names.split()]

        raw_qo = sb("a_raw_qo", [P, C, D])
        raw_kv = sb("a_raw_kv", [P, C, 2 * KVH * HD])
        ctx_raw = sb("ctx_raw", [P, 512])
        wq = [sb(f"a_wq_{x}", [P, C, D], F32R) for x in ("hi", "lo")]
        wkv = [sb(f"a_wkv_{x}", [P, C, 2 * KVH * HD], F32R) for x in ("hi", "lo")]
        wo = [sb(f"a_wo_{x}", [P, G, D], F32R) for x in ("hi", "lo")]
        cos = sb("cos", [P, 2, HD])
        sin = sb("sin", [P, 2, HD])
        mask = sb("mask", [P, G, S], BF16)
        ident16 = sb("ident16", [P, P], BF16)
        stats = sb("a_stats", [P, B, 6])
        moments = sb("a_moments", [P, B, 2])
        rstd = sb("a_rstd", [P, B])
        stats2 = sb("a_stats2", [P, 6])
        moments2 = sb("a_moments2", [P, 2])
        rstd2 = sb("a_rstd2", [P, 1])
        xn = sb("a_xn", [P, D])
        xnT = [sb(f"a_xnT_{x}", [P, C, S], F32R) for x in ("hi", "lo")]
        xn2 = sb("a_xn2", [P, D])
        rot_c = sb("rot_c", [P, H + KVH, HD])
        rot_s = sb("rot_s", [P, H + KVH, HD])
        rot = sb("rot", [P, H + KVH, HD])
        q_stack = sb("q_stack", [P, H, 4, HD], F32R)
        k_stack = sb("k_stack", [P, KVH, 4, 2, HD], F32R)
        qT = sb("a_qT", [P, H // 2, S], F32R)
        kT = sb("a_kT", [P, KVH, 2, S], F32R)
        v_sb = sb("a_v", [P, KVH, HD])
        v_pad = sb("a_v_pad", [P, KVH, KVH * HD + HD])
        neg_max = sb("a_neg_max", [P, 2, G])
        total = sb("a_total", [P, H])
        inv = sb("a_inv", [P, H])
        p = sb("a_p", [P, 2, G, S])
        pT = sb("a_pT", [P, 2, G, S])
        inv_wide = sb("a_inv_wide", [P, G, KVH, HD])
        invT = sb("a_invT", [P, G, S])
        o = sb("a_o", [P, G, S])
        oT = [sb(f"a_oT_{x}", [P, G, S], F32R) for x in ("hi", "lo")]
        acc, xT, cT, ident, minus_half = mem["x"], mem["xT"], mem["cT"], mem["ident"], mem["minus_half"]

        ps_s = [ps(f"a_ps_s{i}") for i in range(2)]
        ps_pT = [ps(f"a_ps_pT{i}") for i in range(2)]
        ps_o = ps("a_ps_o")
        ps_t = ps("a_ps_t")
        ps_u = ps("a_ps_u")
        ps_w = ps("a_ps_w")

        x0_in, x_in, w_in, tab_in, wo_in, ctx_in = signals("x0_in x_in aw_in tab_in awo_in ctx_in")
        (xnT_ps, q_ps, kv_ps, qT_ps, kT_ps, s_ps, pT_ps, pv_ps, invT_ps, y_ps, x2T_ps) = signals(
            "xnT_ps q_ps kv_ps qT_ps kT_ps s_ps pT_ps pv_ps invT_ps y_ps x2T_ps")
        exp_done, xn_hi, q_hi, qT_sb, invT_sb, o_hi, x2_hi = signals("exp_done xn_hi q_hi qT_sb invT_sb o_hi x2_hi")
        (stats_ok, moments_ok, xn_ok, w_hi, w_lo, wo_hi, wo_lo, xn_lo, max_ok, roped, v_ok, v_padded, q_lo) = signals(
            "stats_ok moments_ok xn_ok aw_hi aw_lo awo_hi awo_lo xn_lo max_ok roped v_ok v_padded q_lo")
        (pT_sb, kT_sb, inv_ok, wide_ok, o_ok, o_lo, acc_ok, stats2_ok, moments2_ok, xn2_ok, x2_lo) = signals(
            "pT_sb kT_sb inv_ok wide_ok o_ok o_lo acc_ok stats2_ok moments2_ok xn2_ok x2_lo")
        (zeroed, consts, var_eps, rstd_ok, var2_eps, rstd2_ok, rot_ok, k_hi, k_lo, ctx_hi, ctx_lo) = signals(
            "zeroed consts var_eps rstd_ok var2_eps rstd2_ok rot_ok k_hi k_lo ctx_hi ctx_lo")
        block = ctx.enter_context(nc.Block())

        @block.sync
        def _(sp):
            sp.dma_start(acc[:, 0, :], io["x"][0]).then_inc(x0_in, 16)
            sp.dma_start(raw_qo[:], io["a_wq"]).then_inc(w_in, 16)
            sp.dma_start(raw_kv[:, :, 0:KVH * HD], io["a_wk"]).then_inc(w_in, 16)
            sp.dma_start(raw_kv[:, :, KVH * HD:], io["a_wv"]).then_inc(w_in, 16)
            sp.dma_start(cos[:], io["cos"]).then_inc(tab_in, 16)
            sp.dma_start(sin[:], io["sin"]).then_inc(tab_in, 16)
            sp.dma_start(acc[:, 1:B, :], io["x"][1:B].rearrange("b s d -> s b d")).then_inc(x_in, 16)
            sp.wait_ge(w_lo, 1)
            sp.dma_start(raw_qo[:], io["a_wo"]).then_inc(wo_in, 16)

            def step(n, first, last):
                wait(sp, ctx_lo, n)
                sp.dma_start(ctx_raw[:], io["ctxT"][bass.ds(n, 1)].rearrange("o p w -> p (o w)")).then_inc(ctx_in, 16)

            steps(sp, B, step)

        @block.gpsimd
        def _(pool):
            pool.memset(minus_half[:], -0.5).then_inc(zeroed, 1)
            pool.memset(ident[:], 0.0).then_inc(zeroed, 1)
            pool.memset(mask[:], 0.0).then_inc(zeroed, 1)
            pool.memset(v_pad[:], 0.0).then_inc(zeroed, 1)
            pool.wait_ge(zeroed, 3)
            pool.affine_select(out=ident[:], in_=ident[:], compare_op=ALU.not_equal, fill=1.0, base=0,
                               pattern=[[-1, P]], channel_multiplier=1).then_inc(consts, 1)
            pool.affine_select(out=mask[:], in_=mask[:], compare_op=ALU.is_ge, fill=NEG, base=0,
                               pattern=[[0, G], [-1, S]], channel_multiplier=1).then_inc(consts, 1)
            pool.wait_ge(consts, 1)
            pool.tensor_copy(ident16[:], ident[:]).then_inc(consts, 1)

            pool.wait_ge(moments_ok, 1)
            pool.tensor_scalar(rstd[:, 0:1], moments[:, 0, 1:2], LN_EPS, None, ALU.add).then_inc(var_eps, 1)
            pool.wait_ge(var_eps, 1)
            pool.tensor_tensor(rstd[:, 0:1], rstd[:, 0:1], minus_half[:, 0:1], ALU.pow).then_inc(rstd_ok, 1)
            pool.memset(kT[:].bitcast(F32), 0.0).then_inc(zeroed, 1)

            def rotate(m):
                pool.wait_ge(roped, 2 * m + 2)
                wait(pool, q_lo, m)
                wait(pool, kT_ps, 2 * m)
                pool.tensor_tensor(rot[:], rot_c[:], rot_s[:], ALU.add).then_inc(rot_ok, 1)
                c, s, keys = (t[:, H:, :].unsqueeze(2).broadcast_to([P, KVH, 4, HD]) for t in (rot_c, rot_s, rot))
                pool.tensor_tensor(k_stack[:, :, :, 0, :], c, s, ALU.add).then_inc(k_hi, 1)
                wait_apart(pool, rot_ok, m + 1, zeroed)
                wait_apart(pool, k_hi, m + 1, zeroed)
                pool.tensor_tensor(k_stack[:, :, :, 1, :], keys, f32(k_stack[:, :, :, 0, :]),
                                   ALU.subtract).then_inc(k_lo, 1)

            def rstd_2(n):
                wait_apart(pool, moments2_ok, n + 1, zeroed)
                pool.tensor_scalar(rstd2[:], moments2[:, 1:2], LN_EPS, None, ALU.add).then_inc(var2_eps, 1)
                wait_apart(pool, var2_eps, n + 1, zeroed)
                pool.tensor_tensor(rstd2[:], rstd2[:], minus_half[:, 0:1], ALU.pow).then_inc(rstd2_ok, 1)

            pool.wait_ge(moments_ok, 2)
            pool.tensor_scalar(rstd[:, 1:B], moments[:, 1:B, 1], LN_EPS, None, ALU.add).then_inc(var_eps, 1)
            pool.wait_ge(var_eps, 2)
            pool.tensor_tensor(rstd[:, 1:B], rstd[:, 1:B], minus_half[:, 1:B], ALU.pow).then_inc(rstd_ok, 1)
            rotate(0)

            def step(n, first, last):
                wait_apart(pool, ctx_in, 16 * (n + 1), zeroed)
                hi, lo = (cT[i][:, bass.ds(n * 512, 512)] for i in range(2))
                pool.tensor_copy(hi, ctx_raw[:]).then_inc(ctx_hi, 1)
                wait_apart(pool, ctx_hi, n + 1, zeroed)
                pool.tensor_tensor(lo, ctx_raw[:], f32(hi), ALU.subtract).then_inc(ctx_lo, 1)
                if not first:
                    rstd_2(n - 1)
                if not last:
                    rotate(n + 1)

            steps(pool, B, step)
            rstd_2(B - 1)

        @block.scalar
        def _(act):
            def xn_high(m):
                act.wait_ge(xnT_ps, m + 1)
                act.activation(xnT[0][:], ps_t[:], ACT.Copy).then_inc(xn_hi, 1)

            def queries_high(m):
                act.wait_ge(rot_ok, m + 1)
                wait(act, qT_ps, 4 * m)
                act.activation(q_stack[:, :, 0:2, :], rot[:, 0:H, :].unsqueeze(2).broadcast_to([P, H, 2, HD]),
                               ACT.Copy).then_inc(q_hi, 1)

            def query_tiles(m, i):
                act.wait_ge(qT_ps, 4 * m + i + 1)
                act.activation(qT[:, 4 * i:4 * i + 4, :], (ps_t if i % 2 else ps_u)[:], ACT.Copy).then_inc(qT_sb, 1)

            def exps(n, j):
                act.wait_ge(max_ok, KVH * n + j + 1)
                if j == 0:
                    wait(act, inv_ok, n)
                for g in range(G):
                    e = act.activation(p[:, j % 2, g, :], ps_s[j % 2][:, g * S:(g + 1) * S], ACT.Exp,
                                       bias=neg_max[:, j % 2, g:g + 1], accum_out=total[:, G * j + g:G * j + g + 1])
                e.then_inc(exp_done, 1)

            def inverse_transposed(n):
                act.wait_ge(invT_ps, n + 1)
                act.activation(invT[:], ps_u[:], ACT.Copy).then_inc(invT_sb, 1)

            def output_high(n):
                act.wait_ge(o_ok, n + 1)
                act.activation(oT[0][:], o[:], ACT.Copy).then_inc(o_hi, 1)

            def x2_high(n):
                act.wait_ge(x2T_ps, n + 1)
                act.activation(xT[0][:, :, bass.ds(n * S, S)], ps_t[:].rearrange("p (c s) -> p c s", c=C),
                               ACT.Copy).then_inc(x2_hi, 1)

            xn_high(0)
            queries_high(0)
            for i in range(4):
                query_tiles(0, i)

            def step(n, first, last):
                exps(n, 0)
                for j in range(KVH):
                    if j + 1 < KVH:
                        exps(n, j + 1)
                    if not first:
                        if j == 0:
                            inverse_transposed(n - 1)
                        if j == 1:
                            output_high(n - 1)
                        if j == 5:
                            x2_high(n - 1)
                    if not last:
                        if j == 1:
                            xn_high(n + 1)
                        if j == 4:
                            queries_high(n + 1)
                        for i in {5: (0,), 6: (1, 2), 7: (3,)}.get(j, ()):
                            query_tiles(n + 1, i)

            steps(act, B, step)
            inverse_transposed(B - 1)
            output_high(B - 1)
            x2_high(B - 1)

        @block.vector
        def _(dve):
            def normalised(m):
                dve.wait_ge(rstd_ok, 1 if isinstance(m, int) and m == 0 else 2)
                wait(dve, xnT_ps, m)
                dve.tensor_scalar(xn[:], acc[:, bass.ds(m, 1), :].rearrange("p o d -> p (o d)"), moments[:, bass.ds(m, 1), 0], rstd[:, bass.ds(m, 1)],
                                  ALU.subtract, ALU.mult).then_inc(xn_ok, 1)

            def xn_low(m):
                dve.wait_ge(xn_hi, m + 1)
                dve.tensor_tensor(xnT[1][:], ps_t[:].rearrange("p (c s) -> p c s", c=C), f32(xnT[0][:]),
                                  ALU.subtract).then_inc(xn_lo, 1)

            def rope(m, source, done, lo, hi, which):
                dve.wait_ge(done, m + 1)
                rows = source.rearrange("p (h d) -> p h d", d=HD)

                def table(t, a, b):
                    return t[:, which, a:b].unsqueeze(1).broadcast_to([P, hi - lo, b - a])

                dve.tensor_tensor(rot_c[:, lo:hi, :], rows, table(cos, 0, HD), ALU.mult)
                dve.tensor_tensor(rot_s[:, lo:hi, 0:HALF], rows[:, :, HALF:], table(sin, 0, HALF), ALU.mult)
                dve.tensor_tensor(rot_s[:, lo:hi, HALF:], rows[:, :, 0:HALF], table(sin, HALF, HD),
                                  ALU.mult).then_inc(roped, 1)

            def rope_queries(m):
                wait(dve, rot_ok, m)
                rope(m, ps_u[:], q_ps, 0, H, 0)

            def rope_keys(m):
                rope(m, ps_w[:, 0:KVH * HD], kv_ps, H, H + KVH, 1)
                wait(dve, v_padded, m)
                dve.tensor_copy(v_sb[:], ps_w[:, KVH * HD:2 * KVH * HD].rearrange("p (h d) -> p h d", d=HD)).then_inc(v_ok, 1)

            def queries_low(m):
                dve.wait_ge(q_hi, m + 1)
                dve.tensor_tensor(q_stack[:, :, 2:4, :], rot[:, 0:H, :].unsqueeze(2).broadcast_to([P, H, 2, HD]),
                                  f32(q_stack[:, :, 0:2, :]), ALU.subtract).then_inc(q_lo, 1)

            def key_tiles(m, i):
                dve.wait_ge(kT_ps, 2 * m + i + 1)
                for r in range(2):
                    rows = slice(64 * r, 64 * r + 64)
                    c = dve.tensor_copy(kT[rows, 4 * i:4 * i + 4, r, :],
                                        (ps_u if i else ps_w)[rows, :].rearrange("p (h s) -> p h s", s=S))
                c.then_inc(kT_sb, 1)

            def pad_values(m):
                dve.wait_ge(v_ok, m + 1)
                wait(dve, pv_ps, KVH * m)
                dve.tensor_copy(v_pad[:, :, 0:HD], v_sb[:]).then_inc(v_padded, 1)

            def maxima(n, j):
                dve.wait_ge(s_ps, KVH * n + j + 1)
                dve.tensor_reduce(neg_max[:, j % 2, :], ps_s[j % 2][:].rearrange("p (g s) -> p g s", g=G),
                                  AX.X, ALU.max, negate=True).then_inc(max_ok, 1)

            def probs_transposed(n, j):
                dve.wait_ge(pT_ps, KVH * n + j + 1)
                dve.tensor_copy(pT[:, j % 2], ps_pT[j % 2][:].rearrange("p (g s) -> p g s", g=G)).then_inc(pT_sb, 1)

            def inverse_totals(n):
                dve.wait_ge(exp_done, KVH * (n + 1))
                dve.reciprocal(inv[:], total[:]).then_inc(inv_ok, 1)
                dve.wait_ge(inv_ok, n + 1)
                wait(dve, invT_ps, n)
                dve.tensor_copy(inv_wide[:], inv[:].rearrange("p (j g) -> p g j", g=G).unsqueeze(3)
                                .broadcast_to([P, G, KVH, HD])).then_inc(wide_ok, 1)

            def output(n):
                dve.wait_ge(invT_sb, n + 1)
                wait(dve, o_lo, n)
                dve.tensor_tensor(o[:], ps_o[:].rearrange("p (g s) -> p g s", g=G), invT[:], ALU.mult).then_inc(o_ok, 1)
                dve.wait_ge(o_hi, n + 1)
                dve.tensor_tensor(oT[1][:], o[:], f32(oT[0][:]), ALU.subtract).then_inc(o_lo, 1)

            def residual(n):
                dve.wait_ge(y_ps, n + 1)
                row = acc[:, bass.ds(n, 1), :].rearrange("p o d -> p (o d)")
                dve.tensor_tensor(row, ps_w[:], row, ALU.add).then_inc(acc_ok, 1)
                wait_apart(dve, acc_ok, n + 1, stats_ok)
                dve.bn_stats(stats2[:], row).then_inc(stats2_ok, 1)
                wait_apart(dve, stats2_ok, n + 1, stats_ok)
                dve.bn_aggr(moments2[:], stats2[:]).then_inc(moments2_ok, 1)

            def normalised_2(n):
                dve.wait_ge(rstd2_ok, n + 1)
                wait(dve, x2T_ps, n)
                dve.tensor_scalar(xn2[:], acc[:, bass.ds(n, 1), :].rearrange("p o d -> p (o d)"), moments2[:, 0:1], rstd2[:, 0:1],
                                  ALU.subtract, ALU.mult).then_inc(xn2_ok, 1)

            def x2_low(n):
                dve.wait_ge(x2_hi, n + 1)
                dve.tensor_tensor(xT[1][:, :, bass.ds(n * S, S)], ps_t[:].rearrange("p (c s) -> p c s", c=C),
                                  f32(xT[0][:, :, bass.ds(n * S, S)]), ALU.subtract).then_inc(x2_lo, 1)

            dve.wait_ge(x0_in, 16)
            dve.bn_stats(stats[:, 0, :], acc[:, 0, :]).then_inc(stats_ok, 1)
            dve.wait_ge(stats_ok, 1)
            dve.bn_aggr(moments[:, 0, :], stats[:, 0, :]).then_inc(moments_ok, 1)
            dve.wait_ge(w_in, 48)
            dve.tensor_copy(wq[0][:], raw_qo[:])
            dve.tensor_copy(wkv[0][:], raw_kv[:]).then_inc(w_hi, 1)
            dve.wait_ge(moments_ok, 1)
            normalised(0)
            dve.wait_ge(w_hi, 1)
            dve.tensor_tensor(wq[1][:], raw_qo[:], f32(wq[0][:]), ALU.subtract)
            dve.tensor_tensor(wkv[1][:], raw_kv[:], f32(wkv[0][:]), ALU.subtract).then_inc(w_lo, 1)
            xn_low(0)
            dve.wait_ge(tab_in, 32)
            rope_queries(0)
            rope_keys(0)
            dve.wait_ge(x_in, 16)
            for b in range(1, B):
                s = dve.bn_stats(stats[:, b, :], acc[:, b, :])
            s.then_inc(stats_ok, 1)
            dve.wait_ge(stats_ok, 2)
            for b in range(1, B):
                s = dve.bn_aggr(moments[:, b, :], stats[:, b, :])
            s.then_inc(moments_ok, 1)
            dve.wait_ge(wo_in, 16)
            dve.tensor_copy(wo[0][:], raw_qo[:]).then_inc(wo_hi, 1)
            queries_low(0)
            dve.wait_ge(wo_hi, 1)
            dve.tensor_tensor(wo[1][:], raw_qo[:], f32(wo[0][:]), ALU.subtract).then_inc(wo_lo, 1)
            dve.wait_ge(zeroed, 5)
            for i in range(2):
                key_tiles(0, i)
            pad_values(0)

            def step(n, first, last):
                maxima(n, 0)
                for j in range(KVH):
                    if j + 1 < KVH:
                        maxima(n, j + 1)
                    m = n + 1
                    if j == 0 and not last:
                        normalised(m)
                    if j == 1 and not first:
                        output(n - 1)
                    if j == 1 and not last:
                        xn_low(m)
                    if j == 2 and not last:
                        rope_queries(m)
                    if j == 2 and not first:
                        residual(n - 1)
                    if j == 3 and not last:
                        rope_keys(m)
                    if j == 3 and not first:
                        normalised_2(n - 1)
                    if j == 4 and not last:
                        queries_low(m)
                    if j == 5 and not first:
                        x2_low(n - 1)
                    probs_transposed(n, j)
                    if j == KVH - 1 and not last:
                        for i in range(2):
                            key_tiles(m, i)
                inverse_totals(n)
                if not last:
                    pad_values(n + 1)

            steps(dve, B, step)
            output(B - 1)
            residual(B - 1)
            normalised_2(B - 1)
            x2_low(B - 1)

        @block.tensor
        def _(pe):
            def xn_transposed(m):
                pe.wait_ge(xn_ok, m + 1)
                wait(pe, qT_sb, 4 * m)
                for c in range(C):
                    mm = pe.transpose(ps_t[:, c * S:(c + 1) * S], xn[:, c * P:(c + 1) * P], ident[:])
                mm.then_inc(xnT_ps, 1)

            def project_queries(m):
                pe.wait_ge(xn_hi, m + 1)
                pe.wait_ge(xn_lo, m + 1)
                wait(pe, kT_sb, 2 * m)
                wait(pe, invT_sb, m - 1)
                split_matmuls(pe, ps_u[:], [(xnT[0][:, c, :], xnT[1][:, c, :], wq[0][:, c, :], wq[1][:, c, :])
                                            for c in range(C)]).then_inc(q_ps, 1)

            def project_keys_values(m):
                wait(pe, kT_sb, 2 * m - 1)
                wait(pe, acc_ok, m - 1)
                split_matmuls(pe, ps_w[:, 0:2 * KVH * HD],
                              [(xnT[0][:, c, :], xnT[1][:, c, :], wkv[0][:, c, :], wkv[1][:, c, :])
                               for c in range(C)]).then_inc(kv_ps, 1)

            def query_tiles(m, i):
                if i == 0:
                    pe.wait_ge(roped, 2 * m + 1)
                    pe.wait_ge(q_lo, m + 1)
                if i == 1:
                    pe.wait_ge(xn_lo, m + 1)
                    wait(pe, x2_lo, m - 1)
                if i >= 2:
                    pe.wait_ge(qT_sb, 4 * m + i - 1)
                tile = ps_t if i % 2 else ps_u
                for h in range(4):
                    mm = pe.transpose(tile[:, h * S:(h + 1) * S],
                                      f32(q_stack[:, 8 * i + 2 * h:8 * i + 2 * h + 2].rearrange("p h a d -> p (h a d)")), ident[:])
                mm.then_inc(qT_ps, 1)

            def key_tiles(m, i):
                if i == 0:
                    pe.wait_ge(k_lo, m + 1)
                    pe.wait_ge(v_ok, m + 1)
                else:
                    pe.wait_ge(qT_sb, 4 * m + 3)
                tile = ps_u if i else ps_w
                for h in range(4):
                    mm = pe.transpose(tile[:, h * S:(h + 1) * S],
                                      f32(k_stack[:, 4 * i + h].rearrange("p a b d -> p (a b d)")), ident[:])
                mm.then_inc(kT_ps, 1)

            def scores(n, j):
                pe.wait_ge(qT_sb, 4 * n + j // 2 + 1)
                pe.wait_ge(kT_sb, 2 * n + j // 4 + 1)
                wait(pe, exp_done, KVH * n + j - 1)
                tile = ps_s[j % 2]
                pe.matmul(tile[:], ident16[:], mask[:].rearrange("p g s -> p (g s)"), start=True, stop=False)
                for h in range(2):
                    mm = pe.matmul(tile[:, 2 * h * S:(2 * h + 2) * S], qT[:, 2 * j + h, :],
                                   kT[:, j].rearrange("p r s -> p (r s)"), start=False, stop=h == 1)
                mm.then_inc(s_ps, 1)

            def probs_transposed(n, j):
                pe.wait_ge(exp_done, KVH * n + j + 1)
                wait(pe, pT_sb, KVH * n + j - 1)
                for g in range(G):
                    mm = pe.transpose(ps_pT[j % 2][:, g * S:(g + 1) * S], p[:, j % 2, g, :], ident[:])
                mm.then_inc(pT_ps, 1)

            def values(n, j):
                pe.wait_ge(pT_sb, KVH * n + j + 1)
                if j == 0:
                    pe.wait_ge(v_padded, n + 1)
                    wait(pe, o_ok, n)
                pe.matmul(ps_o[:], v_pad[:].rearrange("p j w -> p (j w)")[:, KVH * HD * j:KVH * HD * (j + 1)],
                          pT[:, j % 2].rearrange("p g s -> p (g s)"), start=j == 0, stop=j == KVH - 1).then_inc(pv_ps, 1)

            def inverse_transposed(n):
                pe.wait_ge(wide_ok, n + 1)
                pe.wait_ge(kT_sb, 2 * n + 2 if isinstance(n, int) and n == B - 1 else 2 * n + 4)
                for g in range(G):
                    mm = pe.transpose(ps_u[:, g * S:(g + 1) * S], inv_wide[:, g].rearrange("p j d -> p (j d)"), ident[:])
                mm.then_inc(invT_ps, 1)

            def project_output(n):
                pe.wait_ge(o_lo, n + 1)
                pe.wait_ge(kT_sb, 2 * n + 1 if isinstance(n, int) and n == B - 1 else 2 * n + 3)
                split_matmuls(pe, ps_w[:], [(oT[0][:, g, :], oT[1][:, g, :], wo[0][:, g, :], wo[1][:, g, :])
                                            for g in range(G)]).then_inc(y_ps, 1)

            def xn2_transposed(n, last):
                pe.wait_ge(xn2_ok, n + 1)
                if last:
                    pe.wait_ge(qT_sb, 4 * B)
                else:
                    pe.wait_ge(xn_lo, n + 3)
                for c in range(C):
                    mm = pe.transpose(ps_t[:, c * S:(c + 1) * S], xn2[:, c * P:(c + 1) * P], ident[:])
                mm.then_inc(x2T_ps, 1)

            pe.wait_ge(consts, 3)
            xn_transposed(0)
            pe.wait_ge(w_lo, 1)
            project_queries(0)
            project_keys_values(0)
            for i in range(4):
                query_tiles(0, i)
            for i in range(2):
                key_tiles(0, i)
            pe.wait_ge(wo_lo, 1)

            def step(n, first, last):
                scores(n, 0)
                for j in range(KVH):
                    if j + 1 < KVH:
                        scores(n, j + 1)
                    m = n + 1
                    if j == 0 and not first:
                        inverse_transposed(n - 1)
                    if j == 1 and not last:
                        xn_transposed(m)
                    if j == 2 and not last:
                        project_queries(m)
                    if j == 2 and not first:
                        project_output(n - 1)
                    if j == 3 and not last:
                        project_keys_values(m)
                    if j == 5 and not first:
                        xn2_transposed(n - 1, last)
                    if not last:
                        if j == 5:
                            query_tiles(m, 0)
                        if j == 6:
                            query_tiles(m, 1)
                            query_tiles(m, 2)
                        if j == 7:
                            query_tiles(m, 3)
                            key_tiles(m, 0)
                            key_tiles(m, 1)
                    probs_transposed(n, j)
                    if j:
                        values(n, j - 1)
                values(n, KVH - 1)

            steps(pe, B, step)
            inverse_transposed(B - 1)
            project_output(B - 1)
            xn2_transposed(B - 1, True)


def cross_attention(nc, mem, io):
    with ExitStack() as ctx:
        def sb(name, shape, dt=F32):
            return ctx.enter_context(nc.sbuf_tensor(name, shape, dt))

        def split(name, shape):
            return [sb(f"{name}_{x}", shape, F32R) for x in ("hi", "lo")]

        def ps(name):
            return ctx.enter_context(nc.psum_tensor(name, [P, 512], F32))

        def signals(names):
            return [ctx.enter_context(nc.semaphore(name)) for name in names.split()]

        NKV = 2 * XD
        raw_wq, raw_wkv, raw_wo = sb("raw_wq", [P, C, XG * XD]), sb("raw_wkv", [P, C, NKV]), sb("raw_wo", [P, XG, D])
        wq, wkv, wo = split("wq", [P, C, XG * XD]), split("wkv", [P, C, NKV]), split("wo", [P, XG, D])
        norm_w = sb("norm_w", [P, 2])
        key_scale = sb("key_scale", [P, 1])
        rms_eps = sb("rms_eps", [P, XG])
        q_sb = sb("q_sb", [P, XG, XD])
        q_squares = sb("q_squares", [P, XG, XD])
        k_squares = sb("k_squares", [P, 2, XD])
        q_mean, k_mean = sb("q_mean", [P, XG]), sb("k_mean", [P, 2])
        q_rms, k_rms = sb("q_rms", [P, XG]), sb("k_rms", [P, 2])
        k_sb = sb("k_sb", [P, 2, XD])
        qT, kT = split("qT", [P, XG, S]), split("kT", [P, KV])
        v = [split(f"v{i}", [P, 2, XD]) for i in range(2)]
        neg_max, bias = sb("neg_max", [P, XG]), sb("bias", [P, XG])
        total, inv = sb("total", [P, XG]), sb("inv", [P, XG])
        p = sb("p", [P, XG, KV])
        pT = split("pT", [P, 2, XG, S])
        oT = split("oT", [P, XG, S])
        acc, xT, cT, ident, minus_half = mem["x"], mem["xT"], mem["cT"], mem["ident"], mem["minus_half"]
        cT = [t[:].rearrange("p (c s) -> p c s", c=C) for t in cT]

        ps_s = [ps(f"ps_s{i}") for i in range(2)]
        ps_q, ps_kv = ps("ps_q"), ps("ps_kv")
        ps_pT = [ps(f"ps_pT{i}") for i in range(2)]
        ps_o, ps_y = ps("ps_o"), ps("ps_y")
        kv_rows = ps_kv[:].rearrange("p (t w) -> p t w", t=2)

        wq_in, wkv_in, wo_in, norm_in, scale_ok, first_lo, eps_ok = signals("wq_in wkv_in wo_in norm_in scale_ok first_lo eps_ok")
        kv_ps, q_ps, s_ps, pT_ps, qT_ps, kT_ps, y_ps, o_ps = signals("b_kv_ps b_q_ps b_s_ps b_pT_ps b_qT_ps b_kT_ps b_y_ps b_o_ps")
        exp_done, k_mean_ok, v_hi, q_ok, q_mean_ok, pT_hi, qT_hi, kT_hi, o_hi = signals(
            "b_exp_done k_mean_ok v_hi q_ok q_mean_ok pT_hi b_qT_hi b_kT_hi b_o_hi")
        max_ok, bias_ok, inv_ok, p_ok, k_ok, v_lo, pT_lo, qT_lo, kT_lo, acc_ok, o_lo = signals(
            "b_max_ok bias_ok b_inv_ok p_ok k_ok v_lo pT_lo b_qT_lo b_kT_lo b_acc_ok b_o_lo")
        k_ms, k_rms_ok, q_ms, q_rms_ok = signals("k_ms k_rms_ok q_ms q_rms_ok")
        wq_hi, wkv_hi, wo_hi, wq_lo, wkv_lo, wo_lo = signals("wq_hi wkv_hi wo_hi wq_lo wkv_lo wo_lo")
        block = ctx.enter_context(nc.Block())

        def heads(eng, body):
            def head(j, first, last):
                for b in range(B):
                    body(j, b, B * j + b, first and b == 0, last and b == B - 1)

            steps(eng, XKVH, head)

        @block.sync
        def _(sp):
            sp.dma_start(norm_w[:, 0:1], io["q_norm"]).then_inc(norm_in, 16)
            sp.dma_start(norm_w[:, 1:2], io["k_norm"]).then_inc(norm_in, 16)

            def load(j):
                for raw, name, landed, used, free in ((raw_wkv, "x_wkv", wkv_in, wkv_lo, j - 1), (raw_wq, "x_wq", wq_in, wq_lo, j - 1),
                                                      (raw_wo, "x_wo", wo_in, wo_lo, j)):
                    wait(sp, used, free)
                    sp.dma_start(raw[:].rearrange("p c n -> p (c n)"),
                                 io[name][bass.ds(j, 1)].rearrange("o p n -> p (o n)")).then_inc(landed, 16)

            load(0)
            sp.wait_ge(first_lo, 2)
            load(1)
            with sp.Fori(2, XKVH) as j:
                load(j)

        @block.gpsimd
        def _(pool):
            def weights_low(j, w, raw, hi, lo):
                pool.wait_ge(hi, j + 1)
                for c in range(C):
                    i = pool.tensor_tensor(w[1][:, c, :], raw[:, c, :], f32(w[0][:, c, :]), ALU.subtract)
                i.then_inc(lo, 1)

            def rms(s, total, summed, out, mean, done):
                pool.wait_ge(summed, s + 1)
                pool.tensor_tensor(out[:], total[:], rms_eps[:, 0:out.shape[1]], ALU.add).then_inc(mean, 1)
                pool.wait_ge(mean, s + 1)
                pool.tensor_tensor(out[:], out[:], minus_half[:, 0:out.shape[1]], ALU.pow).then_inc(done, 1)

            def k_rms_step(s):
                rms(s, k_mean, k_mean_ok, k_rms, k_ms, k_rms_ok)

            def q_rms_step(s):
                rms(s, q_mean, q_mean_ok, q_rms, q_ms, q_rms_ok)

            pool.memset(rms_eps[:], RMS_EPS).then_inc(eps_ok, 1)
            pool.wait_ge(eps_ok, 1)
            k_rms_step(0)
            q_rms_step(0)
            weights_low(0, wo, raw_wo, wo_hi, wo_lo)

            def step(j, b, s, first, last):
                if not last:
                    k_rms_step(s + 1)
                if b == B - 2 and not (isinstance(j, int) and j == XKVH - 1):
                    weights_low(j + 1, wkv, raw_wkv, wkv_hi, wkv_lo)
                    weights_low(j + 1, wq, raw_wq, wq_hi, wq_lo)
                if not last:
                    q_rms_step(s + 1)
                if b == 0 and not first:
                    weights_low(j, wo, raw_wo, wo_hi, wo_lo)

            heads(pool, step)

        @block.scalar
        def _(act):
            def exps(s):
                for g in range(XG):
                    act.wait_ge(bias_ok, 2 * s + g // 2 + 1)
                    act.activation(p[:, g, :], ps_s[g // 2][:, g % 2 * KV:(g % 2 + 1) * KV], ACT.Exp, bias=bias[:, g:g + 1],
                                   scale=q_rms[:, g:g + 1], accum_out=total[:, g:g + 1]).then_inc(exp_done, 1)

            def keys_values(s, b):
                act.wait_ge(kv_ps, s + 1)
                for t in range(2):
                    i = act.activation(k_squares[:, t, :], kv_rows[:, t, 0:XD], ACT.Square, scale=XD ** -0.5,
                                       accum_out=k_mean[:, t:t + 1])
                i.then_inc(k_mean_ok, 1)
                act.activation(v[b % 2][0][:], kv_rows[:, :, XD:], ACT.Copy).then_inc(v_hi, 1)

            def queries(s):
                act.wait_ge(q_ps, s + 1)
                act.activation(q_sb[:], ps_q[:].rearrange("p (g d) -> p g d", g=XG), ACT.Copy).then_inc(q_ok, 1)

            def query_sums(s):
                act.wait_ge(q_ok, s + 1)
                for g in range(XG):
                    i = act.activation(q_squares[:, g, :], q_sb[:, g, :], ACT.Square, scale=XD ** -0.5,
                                       accum_out=q_mean[:, g:g + 1])
                i.then_inc(q_mean_ok, 1)

            def probs_high(s):
                for t in range(2):
                    act.wait_ge(pT_ps, 2 * s + t + 1)
                    act.activation(pT[0][:, t], ps_pT[t][:].rearrange("p (g s) -> p g s", g=XG), ACT.Copy).then_inc(pT_hi, 1)

            def queries_keys_high(s):
                act.wait_ge(qT_ps, s + 1)
                act.activation(qT[0][:], ps_q[:].rearrange("p (g d) -> p g d", g=XG), ACT.Copy).then_inc(qT_hi, 1)
                act.wait_ge(kT_ps, s + 1)
                act.activation(kT[0][:], ps_kv[:, 0:KV], ACT.Copy, scale=key_scale[:, 0:1]).then_inc(kT_hi, 1)

            def output_high(s):
                act.wait_ge(o_ps, s + 1)
                act.activation(oT[0][:], ps_o[:].rearrange("p (g s) -> p g s", g=XG), ACT.Copy).then_inc(o_hi, 1)

            keys_values(0, 0)
            queries(0)
            query_sums(0)
            act.wait_ge(scale_ok, 1)
            queries_keys_high(0)

            def step(j, b, s, first, last):
                exps(s)
                if not last:
                    keys_values(s + 1, b + 1)
                    queries(s + 1)
                probs_high(s)
                if not last:
                    queries_keys_high(s + 1)
                    query_sums(s + 1)
                output_high(s)

            heads(act, step)

        @block.vector
        def _(dve):
            def weights_high(j, w, raw, landed, used, hi):
                dve.wait_ge(landed, 16 * (j + 1))
                wait(dve, used, B * j)
                dve.tensor_copy(w[0][:], raw[:]).then_inc(hi, 1)

            def biases(s):
                for h in range(2):
                    two = slice(2 * h, 2 * h + 2)
                    dve.wait_ge(s_ps, 2 * s + h + 1)
                    dve.tensor_reduce(neg_max[:, two], ps_s[h][:].rearrange("p (g k) -> p g k", g=2), AX.X, ALU.max,
                                      negate=True).then_inc(max_ok, 1)
                    dve.wait_ge(max_ok, 2 * s + h + 1)
                    dve.wait_ge(q_rms_ok, s + 1)
                    dve.tensor_tensor(bias[:, two], neg_max[:, two], q_rms[:, two], ALU.mult).then_inc(bias_ok, 1)

            def probs(s):
                for h in range(2):
                    two = slice(2 * h, 2 * h + 2)
                    dve.wait_ge(exp_done, XG * s + 2 * h + 2)
                    dve.reciprocal(inv[:, two], total[:, two]).then_inc(inv_ok, 1)
                    dve.wait_ge(inv_ok, 2 * s + h + 1)
                    for g in range(2 * h, 2 * h + 2):
                        i = dve.tensor_scalar(p[:, g, :], p[:, g, :], inv[:, g:g + 1], None, ALU.mult)
                    i.then_inc(p_ok, 1)

            def keys_values(s, b):
                dve.wait_ge(v_hi, s + 1)
                dve.tensor_tensor(v[b % 2][1][:], kv_rows[:, :, XD:], f32(v[b % 2][0][:]), ALU.subtract).then_inc(v_lo, 1)
                dve.wait_ge(k_rms_ok, s + 1)
                dve.tensor_tensor(k_sb[:], kv_rows[:, :, 0:XD], k_rms[:].unsqueeze(2).broadcast_to([P, 2, XD]),
                                  ALU.mult).then_inc(k_ok, 1)

            def probs_low(s):
                for t in range(2):
                    dve.wait_ge(pT_hi, 2 * s + t + 1)
                    dve.tensor_tensor(pT[1][:, t], ps_pT[t][:].rearrange("p (g s) -> p g s", g=XG), f32(pT[0][:, t]),
                                      ALU.subtract).then_inc(pT_lo, 1)

            def queries_keys_low(s):
                dve.wait_ge(qT_hi, s + 1)
                dve.tensor_tensor(qT[1][:], ps_q[:].rearrange("p (g d) -> p g d", g=XG), f32(qT[0][:]),
                                  ALU.subtract).then_inc(qT_lo, 1)
                dve.wait_ge(kT_hi, s + 1)
                dve.scalar_tensor_tensor(kT[1][:], ps_kv[:, 0:KV], key_scale[:, 0:1], f32(kT[0][:]), ALU.mult,
                                         ALU.subtract).then_inc(kT_lo, 1)

            def residual(s, b):
                dve.wait_ge(y_ps, s + 1)
                dve.tensor_tensor(acc[:, b, :], ps_y[:], acc[:, b, :], ALU.add).then_inc(acc_ok, 1)

            def output_low(s):
                dve.wait_ge(o_hi, s + 1)
                dve.tensor_tensor(oT[1][:], ps_o[:].rearrange("p (g s) -> p g s", g=XG), f32(oT[0][:]),
                                  ALU.subtract).then_inc(o_lo, 1)

            weights_high(0, wkv, raw_wkv, wkv_in, kv_ps, wkv_hi)
            dve.wait_ge(wkv_hi, 1)
            dve.tensor_tensor(wkv[1][:], raw_wkv[:], f32(wkv[0][:]), ALU.subtract).then_inc(first_lo, 1)
            weights_high(0, wq, raw_wq, wq_in, q_ps, wq_hi)
            dve.wait_ge(wq_hi, 1)
            dve.tensor_tensor(wq[1][:], raw_wq[:], f32(wq[0][:]), ALU.subtract).then_inc(first_lo, 1)
            dve.wait_ge(norm_in, 32)
            dve.scalar_tensor_tensor(key_scale[:], norm_w[:, 0:1], float(XD) ** -0.5, norm_w[:, 1:2], ALU.mult,
                                     ALU.mult).then_inc(scale_ok, 1)
            keys_values(0, 0)
            dve.wait_ge(scale_ok, 1)
            queries_keys_low(0)
            weights_high(0, wo, raw_wo, wo_in, y_ps, wo_hi)

            def step(j, b, s, first, last):
                biases(s)
                probs(s)
                more = b == B - 2 and not (isinstance(j, int) and j == XKVH - 1)
                if not last:
                    keys_values(s + 1, b + 1)
                if more:
                    weights_high(j + 1, wkv, raw_wkv, wkv_in, kv_ps, wkv_hi)
                    weights_high(j + 1, wq, raw_wq, wq_in, q_ps, wq_hi)
                probs_low(s)
                if not last:
                    queries_keys_low(s + 1)
                if not first:
                    residual(s - 1, (b - 1) % B)
                if b == 0 and not first:
                    weights_high(j, wo, raw_wo, wo_in, y_ps, wo_hi)
                output_low(s)

            heads(dve, step)
            residual(XKVH * B - 1, B - 1)

        @block.tensor
        def _(pe):
            def project_keys_values(s, b, j):
                wait(pe, kT_lo, s)
                if not (isinstance(j, int) and j == 0):
                    pe.wait_ge(wkv_lo, j)
                rows = slice(b * S, (b + 1) * S)
                for t, src in enumerate((cT, xT)):
                    mm = split_matmuls(pe, ps_kv[:, t * NKV:(t + 1) * NKV],
                                       [(src[0][:, c, rows], src[1][:, c, rows], wkv[0][:, c, :], wkv[1][:, c, :])
                                        for c in range(C)])
                mm.then_inc(kv_ps, 1)

            def project_queries(s, b, j):
                wait(pe, qT_lo, s)
                if not (isinstance(j, int) and j == 0):
                    pe.wait_ge(wq_lo, j)
                rows = slice(b * S, (b + 1) * S)
                split_matmuls(pe, ps_q[:], [(xT[0][:, c, rows], xT[1][:, c, rows], wq[0][:, c, :], wq[1][:, c, :])
                                            for c in range(C)]).then_inc(q_ps, 1)

            def scores(s):
                pe.wait_ge(qT_lo, s + 1)
                pe.wait_ge(kT_lo, s + 1)
                wait(pe, exp_done, XG * s)
                for g in range(XG):
                    mm = split_matmuls(pe, ps_s[g // 2][:, g % 2 * KV:(g % 2 + 1) * KV],
                                       [(qT[0][:, g, :], qT[1][:, g, :], kT[0][:], kT[1][:])])
                    if g % 2:
                        mm.then_inc(s_ps, 1)

            def probs_transposed(s):
                pe.wait_ge(p_ok, 2 * s + 2)
                wait(pe, pT_lo, 2 * s)
                for t in range(2):
                    for g in range(XG):
                        mm = pe.transpose(ps_pT[t][:, g * S:(g + 1) * S], p[:, g, t * S:(t + 1) * S], ident[:])
                    mm.then_inc(pT_ps, 1)

            def queries_keys_transposed(s):
                pe.wait_ge(q_ok, s + 1)
                for g in range(XG):
                    mm = pe.transpose(ps_q[:, g * S:(g + 1) * S], q_sb[:, g, :], ident[:])
                mm.then_inc(qT_ps, 1)
                pe.wait_ge(v_lo, s + 1)
                pe.wait_ge(k_ok, s + 1)
                for t in range(2):
                    mm = pe.transpose(ps_kv[:, t * S:(t + 1) * S], k_sb[:, t, :], ident[:])
                mm.then_inc(kT_ps, 1)

            def project_output(s, j):
                pe.wait_ge(o_lo, s + 1)
                wait(pe, acc_ok, s)
                pe.wait_ge(wo_lo, j + 1)
                split_matmuls(pe, ps_y[:], [(oT[0][:, g, :], oT[1][:, g, :], wo[0][:, g, :], wo[1][:, g, :])
                                            for g in range(XG)]).then_inc(y_ps, 1)

            def values(s, b):
                pe.wait_ge(pT_lo, 2 * s + 2)
                split_matmuls(pe, ps_o[:], [(v[b % 2][0][:, t, :], v[b % 2][1][:, t, :],
                                             pT[0][:, t].rearrange("p g s -> p (g s)"), pT[1][:, t].rearrange("p g s -> p (g s)"))
                                            for t in range(2)]).then_inc(o_ps, 1)

            pe.wait_ge(first_lo, 1)
            project_keys_values(0, 0, 0)
            pe.wait_ge(first_lo, 2)
            project_queries(0, 0, 0)
            queries_keys_transposed(0)

            def step(j, b, s, first, last):
                scores(s)
                if not last:
                    following = j + 1 if b == B - 1 else j
                    project_keys_values(s + 1, (b + 1) % B, following)
                    project_queries(s + 1, (b + 1) % B, following)
                probs_transposed(s)
                if not last:
                    queries_keys_transposed(s + 1)
                if not first:
                    project_output(s - 1, j - 1 if b == 0 else j)
                values(s, b)

            heads(pe, step)
            project_output(XKVH * B - 1, XKVH - 1)


def linear(nc, mem, io):
    with ExitStack() as ctx:
        def sb(name, shape, dt=F32):
            return ctx.enter_context(nc.sbuf_tensor(name, shape, dt))

        def split(name, shape):
            return [sb(f"{name}_{x}", shape, F32R) for x in ("hi", "lo")]

        def signals(names):
            return [ctx.enter_context(nc.semaphore(name)) for name in names.split()]

        packed = sb("packed", [P, 2, D], I32)
        scale = sb("scale", [P, 2, D])
        bits = sb("bits", [P, 2, 2, D], I32)
        twice = sb("twice", [P, 2, D])
        weights = sb("weights", [P, 2, 2, D])
        w = split("w", [P, C, D])
        bias = sb("f_bias", [P, D])
        stats, moments, rstd = sb("f_stats", [P, B, 6]), sb("f_moments", [P, B, 2]), sb("f_rstd", [P, B])
        xn = sb("f_xn", [P, 2, D])
        xnT = [split(f"f_xnT{i}", [P, C, S]) for i in range(2)]
        base = sb("f_base", [P, 2, D])
        y = sb("f_y", [P, 2, D])
        ps_x = [ctx.enter_context(nc.psum_tensor(f"f_ps_x{i}", [P, 512], F32)) for i in range(2)]
        ps_y = [ctx.enter_context(nc.psum_tensor(f"f_ps_y{i}", [P, 512], F32)) for i in range(2)]
        acc, ident, minus_half = mem["x"], mem["ident"], mem["minus_half"]

        packed_in, scale_in, bias_in, *stored = signals("packed_in scale_in bias_in stored_even stored_odd")
        bits_ok, twice_ok, product_ok, weights_ok, w_hi, w_lo = signals("bits_ok twice_ok product_ok weights_ok fw_hi fw_lo")
        stats_ok, moments_ok, xn_ok, xn_lo, y_ok = signals("f_stats_ok f_moments_ok f_xn_ok f_xn_lo f_y_ok")
        xn_hi, var_eps, rstd_ok, base_ok, xT_ps, y_ps = signals("f_xn_hi f_var_eps f_rstd_ok f_base_ok f_xT_ps f_y_ps")
        block = ctx.enter_context(nc.Block())

        @block.sync
        def _(sp):
            sp.dma_start(packed[:], io["q4"].rearrange("t p o -> p t o")).then_inc(packed_in, 16)
            for t in range(2):
                for g in range(8):
                    sp.dma_start(scale[16 * g:16 * g + 16, t, :],
                                 io["q4_scale"][8 * t + g:8 * t + g + 1, :].broadcast_to([16, D])).then_inc(scale_in, 16)
            sp.dma_start(bias[:], io["bias"].broadcast_to([P, D])).then_inc(bias_in, 16)
            for b in range(B):
                sp.wait_ge(y_ok, b + 1)
                sp.dma_start(io["out"][b], y[:, b % 2, :]).then_inc(stored[b % 2], 16)
            for done in stored:
                sp.wait_ge(done, 16 * B // 2)

        @block.gpsimd
        def _(pool):
            for b in range(B):
                pool.wait_ge(moments_ok, b + 1)
                pool.tensor_scalar(rstd[:, b:b + 1], moments[:, b, 1:2], LN_EPS, None, ALU.add).then_inc(var_eps, 1)
                pool.wait_ge(var_eps, b + 1)
                pool.tensor_tensor(rstd[:, b:b + 1], rstd[:, b:b + 1], minus_half[:, 0:1], ALU.pow).then_inc(rstd_ok, 1)
                if b == 0:
                    pool.wait_ge(bias_in, 16)
                if b >= 2:
                    pool.wait_ge(y_ok, b - 1)
                pool.tensor_tensor(base[:, b % 2, :], acc[:, b, :], bias[:], ALU.add).then_inc(base_ok, 1)

        @block.scalar
        def _(act):
            for b in range(B):
                act.wait_ge(xT_ps, b + 1)
                if b >= 2:
                    act.wait_ge(y_ps, b - 1)
                act.activation(xnT[b % 2][0][:], ps_x[b % 2][:].rearrange("p (c s) -> p c s", c=C), ACT.Copy).then_inc(xn_hi, 1)

        @block.vector
        def _(dve):
            def statistics(b):
                dve.bn_stats(stats[:, b, :], acc[:, b, :]).then_inc(stats_ok, 1)
                dve.wait_ge(stats_ok, b + 1)
                dve.bn_aggr(moments[:, b, :], stats[:, b, :]).then_inc(moments_ok, 1)

            def normalised(b):
                dve.wait_ge(rstd_ok, b + 1)
                if b >= 2:
                    dve.wait_ge(xT_ps, b - 1)
                dve.tensor_scalar(xn[:, b % 2, :], acc[:, b, :], moments[:, b, 0:1], rstd[:, b:b + 1], ALU.subtract,
                                  ALU.mult).then_inc(xn_ok, 1)

            def low(b):
                dve.wait_ge(xn_hi, b + 1)
                dve.tensor_tensor(xnT[b % 2][1][:], ps_x[b % 2][:].rearrange("p (c s) -> p c s", c=C), f32(xnT[b % 2][0][:]),
                                  ALU.subtract).then_inc(xn_lo, 1)

            statistics(0)
            dve.wait_ge(packed_in, 16)
            dve.tensor_scalar(bits[:, 0], packed[:], 15, None, ALU.bitwise_and)
            dve.tensor_scalar(bits[:, 1], packed[:], 4, 15, ALU.logical_shift_right, ALU.bitwise_and).then_inc(bits_ok, 1)
            dve.wait_ge(scale_in, 16 * 16)
            dve.tensor_scalar(twice[:], scale[:], 2.0, None, ALU.mult).then_inc(twice_ok, 1)
            dve.wait_ge(bits_ok, 1)
            dve.wait_ge(twice_ok, 1)
            for h in range(2):
                dve.scalar_tensor_tensor(weights[:, h], bits[:, h], 1.0 / 15.0, twice[:], ALU.mult, ALU.mult).then_inc(product_ok, 1)
            normalised(0)
            for h in range(2):
                dve.wait_ge(product_ok, h + 1)
                dve.tensor_tensor(weights[:, h], weights[:, h], scale[:], ALU.subtract).then_inc(weights_ok, 1)
            low(0)
            dve.wait_ge(weights_ok, 2)
            flat = weights[:].rearrange("p h t o -> p (h t) o")
            dve.tensor_copy(w[0][:], flat).then_inc(w_hi, 1)
            dve.wait_ge(w_hi, 1)
            dve.tensor_tensor(w[1][:], flat, f32(w[0][:]), ALU.subtract).then_inc(w_lo, 1)
            statistics(1)
            for b in range(B):
                if b + 2 < B:
                    statistics(b + 2)
                if b + 1 < B:
                    normalised(b + 1)
                    low(b + 1)
                dve.wait_ge(y_ps, b + 1)
                dve.wait_ge(base_ok, b + 1)
                if b >= 2:
                    dve.wait_ge(stored[b % 2], 16 * (b // 2))
                dve.tensor_tensor(y[:, b % 2, :], ps_y[b % 2][:], base[:, b % 2, :], ALU.add).then_inc(y_ok, 1)

        @block.tensor
        def _(pe):
            def transposed(b):
                pe.wait_ge(xn_ok, b + 1)
                if b >= 2:
                    pe.wait_ge(xn_lo, b - 1)
                for c in range(C):
                    first = 2 * P * (c % 2) + c // 2
                    mm = pe.transpose(ps_x[b % 2][:, c * S:(c + 1) * S], xn[:, b % 2, first:first + 2 * P - 1:2], ident[:])
                mm.then_inc(xT_ps, 1)

            transposed(0)
            for b in range(B):
                if b + 1 < B:
                    transposed(b + 1)
                pe.wait_ge(xn_lo, b + 1)
                pe.wait_ge(w_lo, 1)
                if b >= 2:
                    pe.wait_ge(y_ok, b - 1)
                x = xnT[b % 2]
                split_matmuls(pe, ps_y[b % 2][:], [(x[0][:, c, :], x[1][:, c, :], w[0][:, c, :], w[1][:, c, :])
                                                   for c in range(C)]).then_inc(y_ps, 1)


def build(nc, io):
    with ExitStack() as ctx:
        def sb(name, shape, dt=F32):
            return ctx.enter_context(nc.sbuf_tensor(name, shape, dt))

        mem = {
            "x": sb("x", [P, B, D]),
            "xT": [sb(f"xT_{h}", [P, C, B * S], F32R) for h in ("hi", "lo")],
            "cT": [sb(f"cT_{h}", [P, C * B * S], F32R) for h in ("hi", "lo")],
            "ident": sb("ident", [P, P]),
            "minus_half": sb("minus_half", [P, 16]),
        }
        self_attention(nc, mem, io)
        cross_attention(nc, mem, io)
        linear(nc, mem, io)


def kernel(**inputs):
    import numpy as np
    import concourse.bacc as bacc
    from concourse.bass_utils import run_bass_kernel_spmd as run

    a = {k: np.asarray(v) for k, v in inputs.items()}
    inv_freq = (1.0 / np.float32(10000.0) ** (np.arange(0, HD, 2, dtype=np.float32) / np.float32(HD))).astype(np.float32)
    angle = np.outer(np.arange(S, dtype=np.float32), inv_freq).astype(np.float32)
    cos, sin = np.cos(angle), np.sin(angle)
    cos, sin = np.concatenate([cos, cos], 1), np.concatenate([-sin, sin], 1)
    key_scale = np.float32(1 / np.sqrt(HD))
    laid = {
        "x": a["x"],
        "ctxT": a["ctx_4096"].reshape(B * S, C, P).transpose(1, 2, 0).reshape(C, P, 2, 512).transpose(0, 2, 1, 3).reshape(2 * C, P, 512),
        "a_wq": a["L0_attn_Wq"].T.reshape(C, P, D).transpose(1, 0, 2),
        "a_wk": a["L0_attn_Wk"].T.reshape(C, P, KVH * HD).transpose(1, 0, 2),
        "a_wv": a["L0_attn_Wv"].T.reshape(C, P, KVH * HD).transpose(1, 0, 2),
        "a_wo": a["L0_attn_Wo"].T.reshape(KVH, G, HD, D).transpose(0, 2, 1, 3).reshape(P, G, D),
        "x_wq": a["L0_xattn_Wq"].reshape(C, P, XKVH, XG * XD).transpose(2, 1, 0, 3).reshape(XKVH, P, C * XG * XD),
        "x_wkv": np.concatenate([a[w].reshape(C, P, XKVH, XD).transpose(2, 1, 0, 3) for w in ("L0_xattn_Wk", "L0_xattn_Wv")],
                                3).reshape(XKVH, P, 2 * C * XD),
        "x_wo": a["L0_xattn_Wo"].reshape(XKVH, XG, XD, D).transpose(0, 2, 1, 3).reshape(XKVH, P, XG * D),
        "q4": a["L0_ffn_weight_q4"].reshape(D, 2 * P, 1).transpose(1, 2, 0).reshape(2, P, D),
        "q4_scale": a["L0_ffn_weight_scale"].reshape(D, D // 32).T,
        "bias": a["L0_ffn_bias"].reshape(1, D),
        "q_norm": a["L0_xattn_q_norm_w"].reshape(XD, 1),
        "k_norm": a["L0_xattn_k_norm_w"].reshape(XD, 1),
        "cos": np.stack([cos, cos * key_scale], 1).astype(np.float32),
        "sin": np.stack([sin, sin * key_scale], 1).astype(np.float32),
    }
    nc = bacc.Bacc("TRN2", target_bir_lowering=False, num_devices=1)
    arrays, io = {}, {}
    for name, array in laid.items():
        arrays["in_" + name] = np.ascontiguousarray(array)
        dt = mybir.dt.from_np(array.dtype)
        io[name] = nc.dram_tensor("in_" + name, array.shape, dt, kind="ExternalInput").ap()
    io["out"] = nc.dram_tensor("out_0", (B, S, D), F32, kind="ExternalOutput").ap()
    build(nc, io)
    return run(nc, [arrays], core_ids=[0]).results[0]["out_0"]
```

```python
from contextlib import ExitStack

import concourse.bass as bass
from concourse import mybir

ALU = mybir.AluOpType
ACT = mybir.ActivationFunctionType
AX = mybir.AxisListType
F32 = mybir.dt.float32
F32R = mybir.dt.float32r
BF16 = mybir.dt.bfloat16
I32 = mybir.dt.int32

P = 128
B, S, D = 8, 128, 512
C = D // P
H, KVH, HD = 32, 8, 16
G = H // KVH
HALF = HD // 2
XKVH, XG, XD = 8, 4, 128
KV = 2 * S
LN_EPS, RMS_EPS = 1e-5, 1e-6
NEG = -3.3895313892515355e38
WARM_UP = 24


def wait(eng, sem, count):
    if not (isinstance(count, int) and count <= 0):
        eng.wait_ge(sem, count)


def wait_apart(eng, sem, count, started):
    if not isinstance(count, int):
        count = eng.snap(count)
    eng.wait_ge(started, 1)
    wait(eng, sem, count)


def f32(ap):
    return ap.bitcast(F32)


def steps(eng, count, body):
    body(0)
    with eng.Fori(1, count - 2) as step:
        body(step)
    body(count - 2)
    body(count - 1)


def exists(row):
    return not isinstance(row, int) or 0 <= row < B


def split_matmuls(pe, out, parts, start=True, stop=True):
    terms = [(a, b) for lh, ll, rh, rl in parts for a, b in ((lh, rh), (lh, rl), (ll, rh))]
    for i, (lhsT, rhs) in enumerate(terms):
        mm = pe.matmul(out, lhsT, rhs, start=start and i == 0, stop=stop and i == len(terms) - 1)
    return mm


def self_attention(nc, mem, io):
    with ExitStack() as ctx:
        def sb(name, shape, dt=F32):
            return ctx.enter_context(nc.sbuf_tensor(name, shape, dt))

        def ps(name, shape=(P, 512)):
            return ctx.enter_context(nc.psum_tensor(name, list(shape), F32))

        def signals(names):
            return [ctx.enter_context(nc.semaphore(name)) for name in names.split()]

        norm_w = sb("norm_w", [P, 2])
        ctx_raw = sb("ctx_raw", [P, 512])
        raw_qo, raw_kv, wq, wkv = mem["raw_wq"], mem["raw_wkv"], mem["wq"], mem["wkv"]
        wo = [sb(f"a_wo_{x}", [P, G, D], F32R) for x in ("hi", "lo")]
        cos = sb("cos", [P, 2, HD])
        sin = sb("sin", [P, 2, HD])
        mask = sb("mask", [P, G, S], BF16)
        ident16 = sb("ident16", [P, P], BF16)
        stats = sb("a_stats", [P, B, 6])
        moments = sb("a_moments", [P, B, 2])
        rstd = sb("a_rstd", [P, B])
        stats2 = sb("a_stats2", [P, 6])
        moments2 = sb("a_moments2", [P, 2])
        rstd2 = sb("a_rstd2", [P, 1])
        xn = sb("a_xn", [P, D])
        xnT = [sb(f"a_xnT_{x}", [P, C, S], F32R) for x in ("hi", "lo")]
        xn2 = sb("a_xn2", [P, D])
        rot_c = sb("rot_c", [P, H + KVH, HD])
        rot_s = sb("rot_s", [P, H + KVH, HD])
        rot = sb("rot", [P, H + KVH, HD])
        q_stack = sb("q_stack", [P, H, 4, HD], F32R)
        k_stack = sb("k_stack", [P, KVH, 4, 2, HD], F32R)
        qT = sb("a_qT", [P, H // 2, S], F32R)
        kT = sb("a_kT", [P, KVH, 2, S], F32R)
        v_sb = sb("a_v", [P, KVH, HD])
        v_pad = sb("a_v_pad", [P, KVH, KVH * HD + HD])
        neg_max = sb("a_neg_max", [P, 2, G])
        total = sb("a_total", [P, H])
        inv = sb("a_inv", [P, H])
        p = sb("a_p", [P, 2, G, S])
        pT = sb("a_pT", [P, 2, G, S])
        inv_wide = sb("a_inv_wide", [P, G, KVH, HD])
        invT = sb("a_invT", [P, G, S])
        o = sb("a_o", [P, G, S])
        oT = [sb(f"a_oT_{x}", [P, G, S], F32R) for x in ("hi", "lo")]
        acc, xT, cT, ident, minus_half = mem["x"], mem["xT"], mem["cT"], mem["ident"], mem["minus_half"]

        ps_s = [mem["ps_kv"], mem["ps_q"]]
        ps_pT = [ps(f"a_ps_pT{i}") for i in range(2)]
        ps_o = ps("a_ps_o")
        ps_t = ps("a_ps_t")
        ps_u = ps("a_ps_u")
        ps_w = ps("a_ps_w")

        x0_in, x_in, wkv_in, tab_in, wo_in, ctx_in, *wq_in = signals("x0_in x_in awkv_in tab_in awo_in ctx_in awq0_in awq1_in")
        (xnT_ps, q_ps, kv_ps, qT_ps, kT_ps, s_ps, pT_ps, pv_ps, invT_ps, y_ps, x2T_ps) = signals(
            "xnT_ps q_ps kv_ps qT_ps kT_ps s_ps pT_ps pv_ps invT_ps y_ps x2T_ps")
        exp_done, xn_hi, q_hi, qT_sb, invT_sb, o_hi, x2_hi = signals("exp_done xn_hi q_hi qT_sb invT_sb o_hi x2_hi")
        (stats_ok, moments_ok, xn_ok, w_hi, w_lo, wo_hi, wo_lo, xn_lo, max_ok, roped, v_ok, v_padded, q_lo) = signals(
            "stats_ok moments_ok xn_ok aw_hi aw_lo awo_hi awo_lo xn_lo max_ok roped v_ok v_padded q_lo")
        (pT_sb, kT_sb, inv_ok, wide_ok, o_ok, o_lo, acc_ok, stats2_ok, moments2_ok, xn2_ok, x2_lo) = signals(
            "pT_sb kT_sb inv_ok wide_ok o_ok o_lo acc_ok stats2_ok moments2_ok xn2_ok x2_lo")
        (zeroed, consts, var_eps, rstd_ok, var2_eps, rstd2_ok, rot_ok, k_hi, k_lo, ctx_hi, ctx_lo) = signals(
            "zeroed consts var_eps rstd_ok var2_eps rstd2_ok rot_ok k_hi k_lo ctx_hi ctx_lo")
        wkv_hi, wkv_lo, ident_ok = signals("awkv_hi awkv_lo ident_ok")
        xw_in, xw_hi, xw_lo, norm_in, scale_ok = signals("xw_in xw_hi xw_lo norm_in scale_ok")
        block = ctx.enter_context(nc.Block())

        @block.sync
        def _(sp):
            sp.dma_start(acc[:, 0:2, :], io["x"][0:2].rearrange("b s d -> s b d")).then_inc(x0_in, 16)
            for c in (0, 2):
                sp.dma_start(raw_qo[:, c:c + 2, :], io["a_wq"][:, c:c + 2, :]).then_inc(wq_in[c // 2], 16)
            sp.dma_start(raw_kv[:], io["a_wkv"]).then_inc(wkv_in, 16)
            sp.dma_start(cos[:], io["cos"]).then_inc(tab_in, 16)
            sp.dma_start(sin[:], io["sin"]).then_inc(tab_in, 16)
            sp.dma_start(acc[:, 2:B, :], io["x"][2:B].rearrange("b s d -> s b d")).then_inc(x_in, 16)
            sp.wait_ge(w_lo, 2)
            sp.dma_start(raw_qo[:], io["a_wo"]).then_inc(wo_in, 16)

            def step(n):
                wait(sp, ctx_lo, n)
                sp.dma_start(ctx_raw[:], io["ctxT"][bass.ds(n, 1)].rearrange("o p w -> p (o w)")).then_inc(ctx_in, 16)

                if isinstance(n, int) and n == B - 2:
                    sp.dma_start(norm_w[:, 0:1], io["q_norm"]).then_inc(norm_in, 16)
                    sp.dma_start(norm_w[:, 1:2], io["k_norm"]).then_inc(norm_in, 16)
                    sp.wait_ge(wo_lo, 1)
                    sp.wait_ge(wkv_lo, 1)
                    sp.dma_start(raw_kv[:].rearrange("p c n -> p (c n)"), io["x_wkv"][0]).then_inc(xw_in, 16)
                    sp.dma_start(raw_qo[:].rearrange("p c n -> p (c n)"), io["x_wq"][0]).then_inc(xw_in, 16)

            steps(sp, B, step)

        @block.gpsimd
        def _(pool):
            pool.memset(minus_half[:], -0.5).then_inc(zeroed, 1)
            pool.memset(ident[:], 0.0).then_inc(zeroed, 1)
            pool.wait_ge(zeroed, 2)
            pool.affine_select(out=ident[:], in_=ident[:], compare_op=ALU.not_equal, fill=1.0, base=0,
                               pattern=[[-1, P]], channel_multiplier=1).then_inc(ident_ok, 1)
            pool.memset(mask[:], 0.0).then_inc(zeroed, 1)
            pool.wait_ge(zeroed, 3)
            pool.affine_select(out=mask[:], in_=mask[:], compare_op=ALU.is_ge, fill=NEG, base=0,
                               pattern=[[0, G], [-1, S]], channel_multiplier=1).then_inc(consts, 1)
            pool.wait_ge(ident_ok, 1)
            pool.tensor_copy(ident16[:], ident[:]).then_inc(consts, 1)

            pool.wait_ge(moments_ok, 1)
            pool.tensor_scalar(rstd[:, 0:2], moments[:, 0:2, 1], LN_EPS, None, ALU.add).then_inc(var_eps, 1)
            pool.wait_ge(var_eps, 1)
            pool.tensor_tensor(rstd[:, 0:2], rstd[:, 0:2], minus_half[:, 0:2], ALU.pow).then_inc(rstd_ok, 1)
            pool.wait_ge(wkv_hi, 1)
            pool.tensor_tensor(wkv[1][:], raw_kv[:], f32(wkv[0][:]), ALU.subtract).then_inc(wkv_lo, 1)
            pool.memset(kT[:].bitcast(F32), 0.0).then_inc(zeroed, 1)
            pool.memset(v_pad[:], 0.0).then_inc(zeroed, 1)

            def rotate_queries(m):
                pool.wait_ge(roped, 2 * m + 1)
                wait(pool, q_lo, m)
                pool.tensor_tensor(rot[:, 0:H, :], rot_c[:, 0:H, :], rot_s[:, 0:H, :], ALU.add).then_inc(rot_ok, 1)

            def rotate_keys(m):
                pool.wait_ge(roped, 2 * m + 2)
                wait(pool, kT_ps, 2 * m)
                pool.tensor_tensor(rot[:, H:, :], rot_c[:, H:, :], rot_s[:, H:, :], ALU.add).then_inc(rot_ok, 1)
                c, s, keys = (t[:, H:, :].unsqueeze(2).broadcast_to([P, KVH, 4, HD]) for t in (rot_c, rot_s, rot))
                pool.tensor_tensor(k_stack[:, :, :, 0, :], c, s, ALU.add).then_inc(k_hi, 1)
                wait_apart(pool, rot_ok, 2 * m + 2, zeroed)
                wait_apart(pool, k_hi, m + 1, zeroed)
                pool.tensor_tensor(k_stack[:, :, :, 1, :], keys, f32(k_stack[:, :, :, 0, :]),
                                   ALU.subtract).then_inc(k_lo, 1)

            def rstd_2(n):
                wait_apart(pool, moments2_ok, n + 1, zeroed)
                pool.tensor_scalar(rstd2[:], moments2[:, 1:2], LN_EPS, None, ALU.add).then_inc(var2_eps, 1)
                wait_apart(pool, var2_eps, n + 1, zeroed)
                pool.tensor_tensor(rstd2[:], rstd2[:], minus_half[:, 0:1], ALU.pow).then_inc(rstd2_ok, 1)

            rotate_queries(0)
            rotate_keys(0)
            pool.wait_ge(moments_ok, 2)
            pool.tensor_scalar(rstd[:, 2:B], moments[:, 2:B, 1], LN_EPS, None, ALU.add).then_inc(var_eps, 1)
            pool.wait_ge(var_eps, 2)
            pool.tensor_tensor(rstd[:, 2:B], rstd[:, 2:B], minus_half[:, 2:B], ALU.pow).then_inc(rstd_ok, 1)

            def step(n):
                wait_apart(pool, ctx_in, 16 * (n + 1), zeroed)
                hi, lo = (cT[i][:, bass.ds(n * 512, 512)] for i in range(2))
                pool.tensor_copy(hi, ctx_raw[:]).then_inc(ctx_hi, 1)
                wait_apart(pool, ctx_hi, n + 1, zeroed)
                pool.tensor_tensor(lo, ctx_raw[:], f32(hi), ALU.subtract).then_inc(ctx_lo, 1)
                if exists(n + 1):
                    rotate_queries(n + 1)
                    rotate_keys(n + 1)
                if isinstance(n, int) and n == 0:
                    pool.wait_ge(wo_in, 16)
                    pool.tensor_copy(wo[0][:], raw_qo[:]).then_inc(wo_hi, 1)
                    pool.wait_ge(wo_hi, 1)
                    pool.tensor_tensor(wo[1][:], raw_qo[:], f32(wo[0][:]), ALU.subtract).then_inc(wo_lo, 1)
                if exists(n - 1):
                    rstd_2(n - 1)

                if isinstance(n, int) and n == B - 1:
                    for i, (w, raw) in enumerate(((wkv, raw_kv), (wq, raw_qo))):
                        pool.wait_ge(xw_hi, i + 1)
                        pool.tensor_tensor(w[1][:], raw[:], f32(w[0][:]), ALU.subtract).then_inc(xw_lo, 1)

            steps(pool, B, step)
            rstd_2(B - 1)

        @block.scalar
        def _(act):
            def xn_high(m):
                act.wait_ge(xnT_ps, m + 1)
                act.activation(xnT[0][:], ps_t[:], ACT.Copy).then_inc(xn_hi, 1)

            def queries_high(m):
                act.wait_ge(rot_ok, 2 * m + 1)
                wait(act, qT_ps, 4 * m)
                act.activation(q_stack[:, :, 0:2, :], rot[:, 0:H, :].unsqueeze(2).broadcast_to([P, H, 2, HD]),
                               ACT.Copy).then_inc(q_hi, 1)

            def query_tiles(m, i):
                act.wait_ge(qT_ps, 4 * m + i + 1)
                act.activation(qT[:, 4 * i:4 * i + 4, :], (ps_t if i % 2 else ps_u)[:], ACT.Copy).then_inc(qT_sb, 1)

            def exps(n, j):
                act.wait_ge(max_ok, KVH * n + j + 1)
                if j == 0:
                    wait(act, inv_ok, n)
                for g in range(G):
                    e = act.activation(p[:, j % 2, g, :], ps_s[j % 2][:, g * S:(g + 1) * S], ACT.Exp,
                                       bias=neg_max[:, j % 2, g:g + 1], accum_out=total[:, G * j + g:G * j + g + 1])
                e.then_inc(exp_done, 1)

            def inverse_transposed(n):
                act.wait_ge(invT_ps, n + 1)
                act.activation(invT[:], ps_u[:], ACT.Copy).then_inc(invT_sb, 1)

            def output_high(n):
                act.wait_ge(o_ok, n + 1)
                act.activation(oT[0][:], o[:], ACT.Copy).then_inc(o_hi, 1)

            def x2_high(n):
                act.wait_ge(x2T_ps, n + 1)
                act.activation(xT[0][:, :, bass.ds(n * S, S)], ps_t[:].rearrange("p (c s) -> p c s", c=C),
                               ACT.Copy).then_inc(x2_hi, 1)

            xn_high(0)
            act.wait_ge(wkv_in, 16)
            act.activation(wkv[0][:], raw_kv[:], ACT.Copy).then_inc(wkv_hi, 1)
            xn_high(1)
            queries_high(0)
            for i in range(3):
                query_tiles(0, i)
            exps(0, 0)

            def step(n):
                for j in range(KVH):
                    if j == 0:
                        if exists(n - 1):
                            inverse_transposed(n - 1)
                    if j == 1:
                        if exists(n - 1):
                            output_high(n - 1)
                        query_tiles(n, 3)
                    if j == 3 and exists(n + 1):
                        queries_high(n + 1)
                    if j == 4 and exists(n + 2):
                        xn_high(n + 2)
                    if j in (5, 6, 7) and exists(n + 1):
                        query_tiles(n + 1, j - 5)
                    if j + 1 < KVH:
                        exps(n, j + 1)
                    elif exists(n + 1):
                        exps(n + 1, 0)
                    if j == 7 and exists(n - 1):
                        x2_high(n - 1)

            steps(act, B, step)
            inverse_transposed(B - 1)
            output_high(B - 1)
            x2_high(B - 1)

        @block.vector
        def _(dve):
            def normalised(m):
                dve.wait_ge(rstd_ok, 1 if isinstance(m, int) and m < 2 else 2)
                wait(dve, xnT_ps, m)
                row = acc[:, bass.ds(m, 1), :].rearrange("p o d -> p (o d)")
                dve.tensor_scalar(xn[:], row, moments[:, bass.ds(m, 1), 0], rstd[:, bass.ds(m, 1)],
                                  ALU.subtract, ALU.mult).then_inc(xn_ok, 1)

            def xn_low(m):
                dve.wait_ge(xn_hi, m + 1)
                dve.tensor_tensor(xnT[1][:], ps_t[:].rearrange("p (c s) -> p c s", c=C), f32(xnT[0][:]),
                                  ALU.subtract).then_inc(xn_lo, 1)

            def rope(m, source, done, lo, hi, which):
                dve.wait_ge(done, m + 1)
                rows = source.rearrange("p (h d) -> p h d", d=HD)

                def table(t, a, b):
                    return t[:, which, a:b].unsqueeze(1).broadcast_to([P, hi - lo, b - a])

                dve.tensor_tensor(rot_c[:, lo:hi, :], rows, table(cos, 0, HD), ALU.mult)
                dve.tensor_tensor(rot_s[:, lo:hi, 0:HALF], rows[:, :, HALF:], table(sin, 0, HALF), ALU.mult)
                dve.tensor_tensor(rot_s[:, lo:hi, HALF:], rows[:, :, 0:HALF], table(sin, HALF, HD),
                                  ALU.mult).then_inc(roped, 1)

            def rope_queries(m):
                wait(dve, rot_ok, 2 * m - 1)
                rope(m, ps_u[:], q_ps, 0, H, 0)

            def rope_keys(m):
                wait(dve, k_hi, m)
                rope(m, ps_w[:, 0:KVH * HD], kv_ps, H, H + KVH, 1)
                wait(dve, v_padded, m)
                dve.tensor_copy(v_sb[:], ps_w[:, KVH * HD:2 * KVH * HD].rearrange("p (h d) -> p h d", d=HD)).then_inc(v_ok, 1)

            def queries_low(m):
                dve.wait_ge(q_hi, m + 1)
                dve.tensor_tensor(q_stack[:, :, 2:4, :], rot[:, 0:H, :].unsqueeze(2).broadcast_to([P, H, 2, HD]),
                                  f32(q_stack[:, :, 0:2, :]), ALU.subtract).then_inc(q_lo, 1)

            def key_tiles(m, i):
                dve.wait_ge(kT_ps, 2 * m + i + 1)
                for r in range(2):
                    rows = slice(64 * r, 64 * r + 64)
                    c = dve.tensor_copy(kT[rows, 4 * i:4 * i + 4, r, :],
                                        ps_w[rows, :].rearrange("p (h s) -> p h s", s=S))
                c.then_inc(kT_sb, 1)

            def pad_values(m):
                dve.wait_ge(v_ok, m + 1)
                wait(dve, pv_ps, KVH * m)
                dve.tensor_copy(v_pad[:, :, 0:HD], v_sb[:]).then_inc(v_padded, 1)

            def maxima(n, j):
                dve.wait_ge(s_ps, KVH * n + j + 1)
                dve.tensor_reduce(neg_max[:, j % 2, :], ps_s[j % 2][:].rearrange("p (g s) -> p g s", g=G),
                                  AX.X, ALU.max, negate=True).then_inc(max_ok, 1)

            def probs_transposed(n, j):
                dve.wait_ge(pT_ps, KVH * n + j + 1)
                dve.tensor_copy(pT[:, j % 2], ps_pT[j % 2][:].rearrange("p (g s) -> p g s", g=G)).then_inc(pT_sb, 1)

            def inverse_totals(n):
                dve.wait_ge(exp_done, KVH * (n + 1))
                dve.reciprocal(inv[:], total[:]).then_inc(inv_ok, 1)
                dve.wait_ge(inv_ok, n + 1)
                wait(dve, invT_ps, n)
                dve.tensor_copy(inv_wide[:], inv[:].rearrange("p (j g) -> p g j", g=G).unsqueeze(3)
                                .broadcast_to([P, G, KVH, HD])).then_inc(wide_ok, 1)

            def output(n):
                dve.wait_ge(invT_sb, n + 1)
                dve.wait_ge(pv_ps, KVH * (n + 1))
                dve.tensor_tensor(o[:], ps_o[:].rearrange("p (g s) -> p g s", g=G), invT[:], ALU.mult).then_inc(o_ok, 1)

            def output_low(n):
                dve.wait_ge(o_hi, n + 1)
                dve.tensor_tensor(oT[1][:], o[:], f32(oT[0][:]), ALU.subtract).then_inc(o_lo, 1)

            def residual(n):
                dve.wait_ge(y_ps, n + 1)
                row = acc[:, bass.ds(n, 1), :].rearrange("p o d -> p (o d)")
                dve.tensor_tensor(row, ps_w[:], row, ALU.add).then_inc(acc_ok, 1)

            def statistics_2(n):
                row = acc[:, bass.ds(n, 1), :].rearrange("p o d -> p (o d)")
                wait_apart(dve, acc_ok, n + 1, stats_ok)
                dve.bn_stats(stats2[:], row).then_inc(stats2_ok, 1)
                wait_apart(dve, stats2_ok, n + 1, stats_ok)
                dve.bn_aggr(moments2[:], stats2[:]).then_inc(moments2_ok, 1)

            def normalised_2(n):
                dve.wait_ge(rstd2_ok, n + 1)
                dve.tensor_scalar(xn2[:], acc[:, bass.ds(n, 1), :].rearrange("p o d -> p (o d)"), moments2[:, 0:1], rstd2[:, 0:1],
                                  ALU.subtract, ALU.mult).then_inc(xn2_ok, 1)

            def x2_low(n):
                dve.wait_ge(x2_hi, n + 1)
                dve.tensor_tensor(xT[1][:, :, bass.ds(n * S, S)], ps_t[:].rearrange("p (c s) -> p c s", c=C),
                                  f32(xT[0][:, :, bass.ds(n * S, S)]), ALU.subtract).then_inc(x2_lo, 1)

            dve.wait_ge(x0_in, 16)
            for b in range(2):
                i = dve.bn_stats(stats[:, b, :], acc[:, b, :])
            i.then_inc(stats_ok, 1)
            dve.wait_ge(stats_ok, 1)
            for b in range(2):
                i = dve.bn_aggr(moments[:, b, :], stats[:, b, :])
            i.then_inc(moments_ok, 1)
            normalised(0)
            for c in range(2):
                half = slice(2 * c, 2 * c + 2)
                dve.wait_ge(wq_in[c], 16)
                dve.tensor_copy(wq[0][:, half, :], raw_qo[:, half, :]).then_inc(w_hi, 1)
                if c == 0:
                    xn_low(0)
                dve.wait_ge(w_hi, c + 1)
                dve.tensor_tensor(wq[1][:, half, :], raw_qo[:, half, :], f32(wq[0][:, half, :]), ALU.subtract).then_inc(w_lo, 1)
            normalised(1)
            dve.wait_ge(tab_in, 32)
            rope_queries(0)
            rope_keys(0)
            xn_low(1)
            queries_low(0)
            dve.wait_ge(x_in, 16)

            def statistics(rows):
                for b in rows:
                    dve.bn_stats(stats[:, b, :], acc[:, b, :]).then_inc(stats_ok, 1)

            statistics(range(2, 4))
            dve.wait_ge(zeroed, 5)
            key_tiles(0, 0)
            statistics(range(4, 5))
            maxima(0, 0)
            statistics(range(5, B))
            dve.wait_ge(stats_ok, B - 1)
            for b in range(2, B):
                i = dve.bn_aggr(moments[:, b, :], stats[:, b, :])
            i.then_inc(moments_ok, 1)

            def step(n):
                for j in range(KVH):
                    if j + 1 < KVH:
                        maxima(n, j + 1)
                    else:
                        inverse_totals(n)
                        if exists(n + 1):
                            maxima(n + 1, 0)
                    if j == 4 and exists(n - 1):
                        residual(n - 1)
                    if j == 6 and exists(n + 1):
                        key_tiles(n + 1, 0)
                    probs_transposed(n, j)
                    if j == 0:
                        if exists(n - 1):
                            output(n - 1)
                        pad_values(n)
                        key_tiles(n, 1)
                        if exists(n + 2):
                            normalised(n + 2)
                    if j == 1:
                        if exists(n - 1):
                            output_low(n - 1)
                        if exists(n + 1):
                            rope_queries(n + 1)
                    if j == 2 and exists(n + 1):
                        rope_keys(n + 1)
                    if j == 3:
                        if exists(n + 1):
                            queries_low(n + 1)
                        if exists(n + 2):
                            xn_low(n + 2)
                    if j == 4 and exists(n - 1):
                        statistics_2(n - 1)
                    if j == 5 and exists(n - 1):
                        normalised_2(n - 1)
                    if j == 7 and exists(n - 1):
                        x2_low(n - 1)
                    if j in (1, 2) and isinstance(n, int) and n == B - 1:
                        dve.wait_ge(xw_in, 32)
                        dve.wait_ge(kv_ps, B)
                        w, raw = ((wkv, raw_kv), (wq, raw_qo))[j - 1]
                        dve.tensor_copy(w[0][:], raw[:]).then_inc(xw_hi, 1)
                    if j == 3 and isinstance(n, int) and n == B - 1:
                        dve.wait_ge(norm_in, 32)
                        dve.scalar_tensor_tensor(mem["key_scale"][:], norm_w[:, 0:1], float(XD) ** -0.5, norm_w[:, 1:2],
                                                 ALU.mult, ALU.mult).then_inc(scale_ok, 1)

            steps(dve, B, step)
            output(B - 1)
            output_low(B - 1)
            residual(B - 1)
            statistics_2(B - 1)
            normalised_2(B - 1)
            x2_low(B - 1)

        @block.tensor
        def _(pe):
            def xn_transposed(m):
                pe.wait_ge(xn_ok, m + 1)
                wait(pe, xn_lo, m)
                wait(pe, qT_sb, 4 * m - 4)
                for c in range(C):
                    mm = pe.transpose(ps_t[:, c * S:(c + 1) * S], xn[:, c * P:(c + 1) * P], ident[:])
                mm.then_inc(xnT_ps, 1)

            def project_queries(m):
                pe.wait_ge(xn_hi, m + 1)
                pe.wait_ge(xn_lo, m + 1)
                wait(pe, qT_sb, 4 * m - 1)
                wait(pe, invT_sb, m - 1)
                split_matmuls(pe, ps_u[:], [(xnT[0][:, c, :], xnT[1][:, c, :], wq[0][:, c, :], wq[1][:, c, :])
                                            for c in range(C)]).then_inc(q_ps, 1)

            def project_keys_values(m):
                wait(pe, kT_sb, 2 * m)
                split_matmuls(pe, ps_w[:, 0:2 * KVH * HD],
                              [(xnT[0][:, c, :], xnT[1][:, c, :], wkv[0][:, c, :], wkv[1][:, c, :])
                               for c in range(C)]).then_inc(kv_ps, 1)

            def query_tiles(m, i):
                if i == 0:
                    pe.wait_ge(roped, 2 * m + 1)
                    pe.wait_ge(q_lo, m + 1)
                if i == 1:
                    wait(pe, qT_sb, 4 * m)
                    if exists(m + 1):
                        pe.wait_ge(xn_lo, m + 2)
                if i == 2:
                    pe.wait_ge(qT_sb, 4 * m + 1)
                if i == 3:
                    pe.wait_ge(qT_sb, 4 * m + 2)
                    wait(pe, x2_lo, m - 1)
                tile = ps_t if i % 2 else ps_u
                for h in range(4):
                    pair = q_stack[:, 8 * i + 2 * h:8 * i + 2 * h + 2].rearrange("p h a d -> p (h a d)")
                    mm = pe.transpose(tile[:, h * S:(h + 1) * S], f32(pair), ident[:])
                mm.then_inc(qT_ps, 1)

            def key_tiles(m, i):
                if i == 0:
                    pe.wait_ge(k_lo, m + 1)
                    pe.wait_ge(v_ok, m + 1)
                    wait(pe, acc_ok, m - 1)
                else:
                    pe.wait_ge(kT_sb, 2 * m + 1)
                for h in range(4):
                    mm = pe.transpose(ps_w[:, h * S:(h + 1) * S],
                                      f32(k_stack[:, 4 * i + h].rearrange("p a b d -> p (a b d)")), ident[:])
                mm.then_inc(kT_ps, 1)

            def scores(n, j):
                pe.wait_ge(qT_sb, 4 * n + j // 2 + 1)
                pe.wait_ge(kT_sb, 2 * n + j // 4 + 1)
                wait(pe, exp_done, KVH * n + j - 1)
                tile = ps_s[j % 2]
                pe.matmul(tile[:], ident16[:], mask[:].rearrange("p g s -> p (g s)"), start=True, stop=False)
                for h in range(2):
                    mm = pe.matmul(tile[:, 2 * h * S:(2 * h + 2) * S], qT[:, 2 * j + h, :],
                                   kT[:, j].rearrange("p r s -> p (r s)"), start=False, stop=h == 1)
                mm.then_inc(s_ps, 1)

            def probs_transposed(n, j):
                pe.wait_ge(exp_done, KVH * n + j + 1)
                wait(pe, pT_sb, KVH * n + j - 1)
                for g in range(G):
                    mm = pe.transpose(ps_pT[j % 2][:, g * S:(g + 1) * S], p[:, j % 2, g, :], ident[:])
                mm.then_inc(pT_ps, 1)

            def values(n, j):
                pe.wait_ge(pT_sb, KVH * n + j + 1)
                if j == 0:
                    pe.wait_ge(v_padded, n + 1)
                    wait(pe, o_ok, n)
                pe.matmul(ps_o[:], v_pad[:].rearrange("p j w -> p (j w)")[:, KVH * HD * j:KVH * HD * (j + 1)],
                          pT[:, j % 2].rearrange("p g s -> p (g s)"), start=j == 0, stop=j == KVH - 1).then_inc(pv_ps, 1)

            def inverse_transposed(n):
                pe.wait_ge(wide_ok, n + 1)
                if exists(n + 1):
                    pe.wait_ge(qT_sb, 4 * n + 7)
                else:
                    pe.wait_ge(invT_sb, n)
                for g in range(G):
                    mm = pe.transpose(ps_u[:, g * S:(g + 1) * S], inv_wide[:, g].rearrange("p j d -> p (j d)"), ident[:])
                mm.then_inc(invT_ps, 1)

            def project_output(n):
                pe.wait_ge(wo_lo, 1)
                pe.wait_ge(o_lo, n + 1)
                if exists(n + 2):
                    pe.wait_ge(v_ok, n + 3)
                else:
                    pe.wait_ge(kT_sb, 2 * B)
                    pe.wait_ge(acc_ok, n)
                split_matmuls(pe, ps_w[:], [(oT[0][:, g, :], oT[1][:, g, :], wo[0][:, g, :], wo[1][:, g, :])
                                            for g in range(G)]).then_inc(y_ps, 1)

            def xn2_transposed(n):
                pe.wait_ge(xn2_ok, n + 1)
                if exists(n + 2):
                    pe.wait_ge(qT_sb, 4 * n + 10)
                else:
                    pe.wait_ge(qT_sb, 4 * B)
                    pe.wait_ge(x2_lo, n)
                for c in range(C):
                    mm = pe.transpose(ps_t[:, c * S:(c + 1) * S], xn2[:, c * P:(c + 1) * P], ident[:])
                mm.then_inc(x2T_ps, 1)

            pe.wait_ge(ident_ok, 1)
            for i in range(WARM_UP):
                pe.transpose(ps_w[:, 0:P], ident[:], ident[:])
            xn_transposed(0)
            for i in range(WARM_UP // 2):
                pe.transpose(ps_w[:, 0:P], ident[:], ident[:])
            pe.wait_ge(xn_hi, 1)
            pe.wait_ge(xn_lo, 1)
            for half in range(2):
                pe.wait_ge(w_lo, half + 1)
                mm = split_matmuls(pe, ps_u[:], [(xnT[0][:, c, :], xnT[1][:, c, :], wq[0][:, c, :], wq[1][:, c, :])
                                                 for c in (2 * half, 2 * half + 1)], start=half == 0, stop=half == 1)
            mm.then_inc(q_ps, 1)
            pe.wait_ge(wkv_lo, 1)
            project_keys_values(0)
            xn_transposed(1)
            pe.wait_ge(consts, 2)
            query_tiles(0, 0)
            query_tiles(0, 1)
            key_tiles(0, 0)
            query_tiles(0, 2)
            scores(0, 0)
            key_tiles(0, 1)

            def step(n):
                for j in range(KVH):
                    if j + 1 < KVH:
                        scores(n, j + 1)
                    elif exists(n + 1):
                        scores(n + 1, 0)
                    probs_transposed(n, j)
                    if j:
                        values(n, j - 1)
                    elif exists(n - 1):
                        values(n - 1, KVH - 1)
                    if j == 0 and exists(n + 1):
                        project_queries(n + 1)
                    if j == 1 and exists(n + 1):
                        project_keys_values(n + 1)
                    if j == 2 and exists(n + 2):
                        xn_transposed(n + 2)
                    if j == 3 and exists(n - 1):
                        project_output(n - 1)
                    if j == 0:
                        query_tiles(n, 3)
                    if j in (4, 5, 6) and exists(n + 1):
                        query_tiles(n + 1, j - 4)
                    if j in (5, 7) and exists(n + 1):
                        key_tiles(n + 1, (j - 5) // 2)
                    if j == 6 and exists(n - 1):
                        xn2_transposed(n - 1)
                    if j == 7:
                        inverse_transposed(n)

            steps(pe, B, step)
            values(B - 1, KVH - 1)
            pe.wait_ge(exp_done, KVH * B)
            pe.wait_ge(ctx_lo, B)
            pe.wait_ge(xw_lo, 2)
            for t, src in enumerate((cT, xT)):
                rows = [s[:].rearrange("p (c s) -> p c s", c=C) if s is cT[i] else s for i, s in enumerate(src)]
                mm = split_matmuls(pe, mem["ps_kv"][:, t * 2 * XD:(t + 1) * 2 * XD],
                                   [(rows[0][:, c, 0:S], rows[1][:, c, 0:S], wkv[0][:, c, :], wkv[1][:, c, :])
                                    for c in range(C)])
            mm.then_inc(mem["kv_ps"], 1)
            project_output(B - 1)
            split_matmuls(pe, mem["ps_q"][:], [(xT[0][:, c, 0:S], xT[1][:, c, 0:S], wq[0][:, c, :], wq[1][:, c, :])
                                               for c in range(C)]).then_inc(mem["q_ps"], 1)
            xn2_transposed(B - 1)




def cross_attention_and_linear(nc, mem, io):
    with ExitStack() as ctx:
        def sb(name, shape, dt=F32):
            return ctx.enter_context(nc.sbuf_tensor(name, shape, dt))

        def split(name, shape):
            return [sb(f"{name}_{x}", shape, F32R) for x in ("hi", "lo")]

        def ps(name):
            return ctx.enter_context(nc.psum_tensor(name, [P, 512], F32))

        def signals(names):
            return [ctx.enter_context(nc.semaphore(name)) for name in names.split()]

        NKV = 2 * XD
        raw_wq, raw_wkv, raw_wo = mem["raw_wq"], mem["raw_wkv"], sb("raw_wo", [P, XG, D])
        wq, wkv, wo = mem["wq"], mem["wkv"], split("wo", [P, XG, D])
        key_scale = mem["key_scale"]
        rms_eps = sb("rms_eps", [P, XG])
        q_sb = sb("q_sb", [P, XG, XD])
        q_squares = sb("q_squares", [P, XG, XD])
        k_squares = sb("k_squares", [P, 2, XD])
        q_mean, k_mean = sb("q_mean", [P, XG]), sb("k_mean", [P, 2])
        q_rms, k_rms = sb("q_rms", [P, XG]), sb("k_rms", [P, 2])
        k_sb = sb("k_sb", [P, 2, XD])
        qT, kT = split("qT", [P, XG, S]), split("kT", [P, KV])
        v = [split(f"v{i}", [P, 2, XD]) for i in range(2)]
        neg_max, bias = sb("neg_max", [P, XG]), sb("bias", [P, XG])
        total, inv = sb("total", [P, XG]), sb("inv", [P, XG])
        p = sb("p", [P, XG, KV])
        pT = split("pT", [P, 2, XG, S])
        oT = split("oT", [P, XG, S])
        packed, scale = raw_wq[:, 0:2, :].bitcast(I32), raw_wq[:, 2:4, :]
        bits = raw_wo[:].rearrange("p (h t) o -> p h t o", h=2).bitcast(I32)
        weights = raw_wo[:].rearrange("p (h t) o -> p h t o", h=2)
        twice = raw_wkv[:].rearrange("p c n -> p (c n)").rearrange("p (t o) -> p t o", o=D)
        xn = twice
        w = split("f_w", [P, C, D])
        f_bias = sb("f_bias", [P, D])
        stats, moments, rstd = sb("f_stats", [P, B, 6]), sb("f_moments", [P, B, 2]), sb("f_rstd", [P, B])
        xnT = [[wkv[x][:, :, i * S:(i + 1) * S] for x in range(2)] for i in range(2)]
        base, y = (raw_wq[:, 2 * i:2 * i + 2, :] for i in range(2))
        acc, xT, cT, ident, minus_half = mem["x"], mem["xT"], mem["cT"], mem["ident"], mem["minus_half"]
        cT = [t[:].rearrange("p (c s) -> p c s", c=C) for t in cT]

        ps_s = [ps(f"ps_s{i}") for i in range(2)]
        ps_q, ps_kv = mem["ps_q"], mem["ps_kv"]
        ps_pT = [ps(f"ps_pT{i}") for i in range(2)]
        ps_o, ps_y = ps("ps_o"), ps("ps_y")
        ps_xn = [ps_pT[0] if b % 2 == 0 and b else ps_kv for b in range(B)]
        ps_f = [ps_s[0] if b % 2 else ps_q for b in range(B)]
        kv_rows = ps_kv[:].rearrange("p (t w) -> p t w", t=2)

        wq_in, wkv_in, wo_in, eps_ok = signals("wq_in wkv_in wo_in eps_ok")
        kv_ps, q_ps = mem["kv_ps"], mem["q_ps"]
        s_ps, pT_ps, qT_ps, kT_ps, y_ps, o_ps = signals("b_s_ps b_pT_ps b_qT_ps b_kT_ps b_y_ps b_o_ps")
        exp_done, k_mean_ok, v_hi, q_ok, q_mean_ok, pT_hi, qT_hi, kT_hi, o_hi = signals(
            "b_exp_done k_mean_ok v_hi q_ok q_mean_ok pT_hi b_qT_hi b_kT_hi b_o_hi")
        max_ok, bias_ok, inv_ok, p_ok, k_ok, v_lo, pT_lo, qT_lo, kT_lo, acc_ok, o_lo = signals(
            "b_max_ok bias_ok b_inv_ok p_ok k_ok v_lo pT_lo b_qT_lo b_kT_lo b_acc_ok b_o_lo")
        k_ms, k_rms_ok, q_ms, q_rms_ok = signals("k_ms k_rms_ok q_ms q_rms_ok")
        wq_hi, wkv_hi, wo_hi, wq_lo, wkv_lo, wo_lo = signals("wq_hi wkv_hi wo_hi wq_lo wkv_lo wo_lo")
        packed_in, scale_in, bias_in, bits_ok, twice_ok, product_ok, weights_ok, w_hi, w_lo = signals(
            "packed_in scale_in bias_in bits_ok twice_ok product_ok weights_ok fw_hi fw_lo")
        stats_ok, moments_ok, xn_ok, xn_lo, out_ok = signals("f_stats_ok f_moments_ok f_xn_ok f_xn_lo f_out_ok")
        xn_hi, var_eps, rstd_ok, base_ok, xnT_ps, f_ps = signals("f_xn_hi f_var_eps f_rstd_ok f_base_ok f_xT_ps f_ps")
        stored = signals("stored_even stored_odd")
        block = ctx.enter_context(nc.Block())

        def heads(eng, body):
            def head(j, first, last):
                for b in range(B):
                    body(j, b, B * j + b, first and b == 0, last and b == B - 1)

            head(0, True, False)
            with eng.Fori(1, XKVH - 1) as j:
                head(j, False, False)
            head(XKVH - 1, False, True)

        @block.sync
        def _(sp):
            def load(raw, name, landed, j):
                sp.dma_start(raw[:].rearrange("p c n -> p (c n)"),
                             io[name][bass.ds(j, 1)].rearrange("o p n -> p (o n)")).then_inc(landed, 16)

            load(raw_wo, "x_wo", wo_in, 0)
            load(raw_wkv, "x_wkv", wkv_in, 1)
            load(raw_wq, "x_wq", wq_in, 1)
            sp.wait_ge(wo_lo, 1)
            load(raw_wo, "x_wo", wo_in, 1)
            with sp.Fori(2, XKVH) as j:
                sp.wait_ge(wkv_lo, j - 1)
                load(raw_wkv, "x_wkv", wkv_in, j)
                sp.wait_ge(wq_lo, j - 1)
                load(raw_wq, "x_wq", wq_in, j)
                sp.wait_ge(wo_lo, j)
                load(raw_wo, "x_wo", wo_in, j)
            sp.wait_ge(wq_lo, XKVH - 1)
            sp.dma_start(packed, io["q4"].rearrange("t p o -> p t o")).then_inc(packed_in, 16)
            for t in range(2):
                for g in range(8):
                    sp.dma_start(scale[16 * g:16 * g + 16, t, :],
                                 io["q4_scale"][8 * t + g:8 * t + g + 1, :].broadcast_to([16, D])).then_inc(scale_in, 16)
            sp.dma_start(f_bias[:], io["bias"].broadcast_to([P, D])).then_inc(bias_in, 16)
            for b in range(B):
                sp.wait_ge(out_ok, b + 1)
                sp.dma_start(io["out"][b], y[:, b % 2, :]).then_inc(stored[b % 2], 16)
            for done in stored:
                sp.wait_ge(done, 16 * B // 2)

        @block.gpsimd
        def _(pool):
            def weights_low(w, raw, hi, lo, count):
                pool.wait_ge(hi, count)
                for c in range(C):
                    i = pool.tensor_tensor(w[1][:, c, :], raw[:, c, :], f32(w[0][:, c, :]), ALU.subtract)
                i.then_inc(lo, 1)

            def rms(s, total, summed, out, mean, done):
                pool.wait_ge(summed, s + 1)
                pool.tensor_tensor(out[:], total[:], rms_eps[:, 0:out.shape[1]], ALU.add).then_inc(mean, 1)
                pool.wait_ge(mean, s + 1)
                pool.tensor_tensor(out[:], out[:], minus_half[:, 0:out.shape[1]], ALU.pow).then_inc(done, 1)

            def k_rms_step(s):
                rms(s, k_mean, k_mean_ok, k_rms, k_ms, k_rms_ok)

            def q_rms_step(s):
                rms(s, q_mean, q_mean_ok, q_rms, q_ms, q_rms_ok)

            pool.memset(rms_eps[:], RMS_EPS).then_inc(eps_ok, 1)
            pool.wait_ge(eps_ok, 1)
            k_rms_step(0)
            q_rms_step(0)
            def step(j, b, s, first, last):
                if not last:
                    k_rms_step(s + 1)
                if b == B - 2 and not (isinstance(j, int) and j == XKVH - 1):
                    weights_low(wkv, raw_wkv, wkv_hi, wkv_lo, j + 1)
                if not last:
                    q_rms_step(s + 1)
                if b == B - 2 and not (isinstance(j, int) and j == XKVH - 1):
                    weights_low(wq, raw_wq, wq_hi, wq_lo, j + 1)
                if b == 0:
                    weights_low(wo, raw_wo, wo_hi, wo_lo, j + 1)
                if isinstance(j, int) and j == XKVH - 1:
                    linear_weights(b)
                    if b:
                        row_rstd(b - 1)

            def linear_weights(b):
                if b == 1:
                    pool.wait_ge(scale_in, 16 * 16)
                    pool.wait_ge(wkv_lo, XKVH - 1)
                    for t in range(2):
                        i = pool.tensor_tensor(twice[:, t, :], scale[:, t, :], scale[:, t, :], ALU.add)
                    i.then_inc(twice_ok, 1)
                if b in (3, 4):
                    h = b - 3
                    pool.wait_ge(product_ok, h + 1)
                    pool.tensor_tensor(weights[:, h], weights[:, h], scale, ALU.subtract).then_inc(weights_ok, 1)
                if b in (5, 6):
                    h = b - 5
                    pool.wait_ge(w_hi, h + 1)
                    pool.tensor_tensor(w[1][:, 2 * h:2 * h + 2, :], weights[:, h], f32(w[0][:, 2 * h:2 * h + 2, :]),
                                       ALU.subtract).then_inc(w_lo, 1)

            def row_rstd(b):
                pool.wait_ge(moments_ok, b + 1)
                pool.tensor_scalar(rstd[:, b:b + 1], moments[:, b, 1:2], LN_EPS, None, ALU.add).then_inc(var_eps, 1)
                pool.wait_ge(var_eps, b + 1)
                pool.tensor_tensor(rstd[:, b:b + 1], rstd[:, b:b + 1], minus_half[:, 0:1], ALU.pow).then_inc(rstd_ok, 1)

            def row_and_bias(b):
                if b == 0:
                    pool.wait_ge(bias_in, 16)
                    pool.wait_ge(bits_ok, 1)
                    pool.wait_ge(weights_ok, 2)
                if b >= 2:
                    pool.wait_ge(out_ok, b - 1)
                pool.tensor_tensor(base[:, b % 2, :], acc[:, b, :], f_bias[:], ALU.add).then_inc(base_ok, 1)

            heads(pool, step)
            for b in range(B):
                if b == 2:
                    row_rstd(B - 1)
                row_and_bias(b)

        @block.scalar
        def _(act):
            def exps(s):
                for g in range(XG):
                    act.wait_ge(bias_ok, 2 * s + g // 2 + 1)
                    act.activation(p[:, g, :], ps_s[g // 2][:, g % 2 * KV:(g % 2 + 1) * KV], ACT.Exp, bias=bias[:, g:g + 1],
                                   scale=q_rms[:, g:g + 1], accum_out=total[:, g:g + 1]).then_inc(exp_done, 1)

            def keys_values(s, b):
                act.wait_ge(kv_ps, s + 1)
                for t in range(2):
                    i = act.activation(k_squares[:, t, :], kv_rows[:, t, 0:XD], ACT.Square, scale=XD ** -0.5,
                                       accum_out=k_mean[:, t:t + 1])
                i.then_inc(k_mean_ok, 1)
                act.activation(v[b % 2][0][:], kv_rows[:, :, XD:], ACT.Copy).then_inc(v_hi, 1)

            def queries(s):
                act.wait_ge(q_ps, s + 1)
                act.activation(q_sb[:], ps_q[:].rearrange("p (g d) -> p g d", g=XG), ACT.Copy).then_inc(q_ok, 1)

            def query_sums(s):
                act.wait_ge(q_ok, s + 1)
                for g in range(XG):
                    i = act.activation(q_squares[:, g, :], q_sb[:, g, :], ACT.Square, scale=XD ** -0.5,
                                       accum_out=q_mean[:, g:g + 1])
                i.then_inc(q_mean_ok, 1)

            def probs_high(s):
                for t in range(2):
                    act.wait_ge(pT_ps, 2 * s + t + 1)
                    act.activation(pT[0][:, t], ps_pT[t][:].rearrange("p (g s) -> p g s", g=XG), ACT.Copy).then_inc(pT_hi, 1)

            def queries_keys_high(s):
                act.wait_ge(qT_ps, s + 1)
                act.activation(qT[0][:], ps_q[:].rearrange("p (g d) -> p g d", g=XG), ACT.Copy).then_inc(qT_hi, 1)
                act.wait_ge(kT_ps, s + 1)
                act.activation(kT[0][:], ps_kv[:, 0:KV], ACT.Copy, scale=key_scale[:, 0:1]).then_inc(kT_hi, 1)

            def output_high(s):
                act.wait_ge(o_ps, s + 1)
                act.activation(oT[0][:], ps_o[:].rearrange("p (g s) -> p g s", g=XG), ACT.Copy).then_inc(o_hi, 1)

            queries(0)
            keys_values(0, 0)
            queries_keys_high(0)
            query_sums(0)

            def xn_high(b):
                act.wait_ge(xnT_ps, b + 1)
                if b >= 2:
                    act.wait_ge(f_ps, b - 1)
                act.activation(xnT[b % 2][0], ps_xn[b][:].rearrange("p (c s) -> p c s", c=C), ACT.Copy).then_inc(xn_hi, 1)

            def step(j, b, s, first, last):
                if last:
                    xn_high(0)
                exps(s)
                if not last:
                    keys_values(s + 1, b + 1)
                    queries(s + 1)
                probs_high(s)
                if not last:
                    queries_keys_high(s + 1)
                    query_sums(s + 1)
                if last:
                    xn_high(1)
                output_high(s)
                if isinstance(j, int) and j == XKVH - 1 and b in (4, 5):
                    h = b - 4
                    act.wait_ge(weights_ok, h + 1)
                    act.activation(w[0][:, 2 * h:2 * h + 2, :], weights[:, h], ACT.Copy).then_inc(w_hi, 1)

            heads(act, step)
            for b in range(2, B):
                xn_high(b)

        @block.vector
        def _(dve):
            def weights_high(j, w, raw, landed, count, used, hi):
                dve.wait_ge(landed, 16 * count)
                wait(dve, used, B * j)
                dve.tensor_copy(w[0][:], raw[:]).then_inc(hi, 1)

            def biases(s):
                for h in range(2):
                    two = slice(2 * h, 2 * h + 2)
                    dve.wait_ge(s_ps, 2 * s + h + 1)
                    dve.tensor_reduce(neg_max[:, two], ps_s[h][:].rearrange("p (g k) -> p g k", g=2), AX.X, ALU.max,
                                      negate=True).then_inc(max_ok, 1)
                    dve.wait_ge(max_ok, 2 * s + h + 1)
                    dve.wait_ge(q_rms_ok, s + 1)
                    dve.tensor_tensor(bias[:, two], neg_max[:, two], q_rms[:, two], ALU.mult).then_inc(bias_ok, 1)

            def probs(s):
                for h in range(2):
                    two = slice(2 * h, 2 * h + 2)
                    dve.wait_ge(exp_done, XG * s + 2 * h + 2)
                    dve.reciprocal(inv[:, two], total[:, two]).then_inc(inv_ok, 1)
                    dve.wait_ge(inv_ok, 2 * s + h + 1)
                    for g in range(2 * h, 2 * h + 2):
                        i = dve.tensor_scalar(p[:, g, :], p[:, g, :], inv[:, g:g + 1], None, ALU.mult)
                    i.then_inc(p_ok, 1)

            def keys_values(s, b):
                dve.wait_ge(v_hi, s + 1)
                dve.tensor_tensor(v[b % 2][1][:], kv_rows[:, :, XD:], f32(v[b % 2][0][:]), ALU.subtract).then_inc(v_lo, 1)
                dve.wait_ge(k_rms_ok, s + 1)
                dve.tensor_tensor(k_sb[:], kv_rows[:, :, 0:XD], k_rms[:].unsqueeze(2).broadcast_to([P, 2, XD]),
                                  ALU.mult).then_inc(k_ok, 1)

            def probs_low(s):
                for t in range(2):
                    dve.wait_ge(pT_hi, 2 * s + t + 1)
                    dve.tensor_tensor(pT[1][:, t], ps_pT[t][:].rearrange("p (g s) -> p g s", g=XG), f32(pT[0][:, t]),
                                      ALU.subtract).then_inc(pT_lo, 1)

            def queries_keys_low(s):
                dve.wait_ge(qT_hi, s + 1)
                dve.tensor_tensor(qT[1][:], ps_q[:].rearrange("p (g d) -> p g d", g=XG), f32(qT[0][:]),
                                  ALU.subtract).then_inc(qT_lo, 1)
                dve.wait_ge(kT_hi, s + 1)
                dve.scalar_tensor_tensor(kT[1][:], ps_kv[:, 0:KV], key_scale[:, 0:1], f32(kT[0][:]), ALU.mult,
                                         ALU.subtract).then_inc(kT_lo, 1)

            def residual(s, b):
                dve.wait_ge(y_ps, s + 1)
                dve.tensor_tensor(acc[:, b, :], ps_y[:], acc[:, b, :], ALU.add).then_inc(acc_ok, 1)

            def output_low(s):
                dve.wait_ge(o_hi, s + 1)
                dve.tensor_tensor(oT[1][:], ps_o[:].rearrange("p (g s) -> p g s", g=XG), f32(oT[0][:]),
                                  ALU.subtract).then_inc(o_lo, 1)

            keys_values(0, 0)
            queries_keys_low(0)

            def linear_bits(b):
                if b == 2:
                    dve.wait_ge(packed_in, 16)
                    dve.wait_ge(wo_lo, XKVH)
                    dve.tensor_scalar(bits[:, 0], packed, 15, None, ALU.bitwise_and)
                    dve.tensor_scalar(bits[:, 1], packed, 4, 15, ALU.logical_shift_right, ALU.bitwise_and).then_inc(bits_ok, 1)
                if b in (3, 4):
                    h = b - 3
                    dve.wait_ge(bits_ok, 1)
                    dve.wait_ge(twice_ok, 1)
                    dve.scalar_tensor_tensor(weights[:, h], bits[:, h], 1.0 / 15.0, twice, ALU.mult,
                                             ALU.mult).then_inc(product_ok, 1)

            def statistics(b):
                dve.wait_ge(acc_ok, (XKVH - 1) * B + b + 1)
                dve.bn_stats(stats[:, b, :], acc[:, b, :]).then_inc(stats_ok, 1)
                dve.wait_ge(stats_ok, b + 1)
                dve.bn_aggr(moments[:, b, :], stats[:, b, :]).then_inc(moments_ok, 1)

            def normalised(b):
                dve.wait_ge(rstd_ok, b + 1)
                if b == 0:
                    dve.wait_ge(product_ok, 2)
                if b >= 2:
                    dve.wait_ge(xnT_ps, b - 1)
                dve.tensor_scalar(xn[:, b % 2, :], acc[:, b, :], moments[:, b, 0:1], rstd[:, b:b + 1], ALU.subtract,
                                  ALU.mult).then_inc(xn_ok, 1)

            def xn_low(b):
                dve.wait_ge(xn_hi, b + 1)
                dve.tensor_tensor(xnT[b % 2][1], ps_xn[b][:].rearrange("p (c s) -> p c s", c=C), f32(xnT[b % 2][0]),
                                  ALU.subtract).then_inc(xn_lo, 1)

            def out_row(b):
                dve.wait_ge(f_ps, b + 1)
                dve.wait_ge(base_ok, b + 1)
                if b >= 2:
                    dve.wait_ge(stored[b % 2], 16 * (b // 2))
                dve.tensor_tensor(y[:, b % 2, :], ps_f[b][:], base[:, b % 2, :], ALU.add).then_inc(out_ok, 1)

            def step(j, b, s, first, last):
                biases(s)
                if last:
                    xn_low(0)
                    normalised(1)
                probs(s)
                more = b == B - 2 and not (isinstance(j, int) and j == XKVH - 1)
                if not last:
                    keys_values(s + 1, b + 1)
                if more:
                    weights_high(j + 1, wkv, raw_wkv, wkv_in, j + 1, kv_ps, wkv_hi)
                    weights_high(j + 1, wq, raw_wq, wq_in, j + 1, q_ps, wq_hi)
                probs_low(s)
                if not last:
                    queries_keys_low(s + 1)
                if not first:
                    residual(s - 1, (b - 1) % B)
                if b == 0:
                    weights_high(j, wo, raw_wo, wo_in, j + 1, y_ps, wo_hi)
                if isinstance(j, int) and j == XKVH - 1:
                    if b:
                        statistics(b - 1)
                    linear_bits(b)
                    if b == B - 2:
                        normalised(0)
                if last:
                    normalised(2)
                    xn_low(1)
                output_low(s)

            heads(dve, step)
            out_row(0)
            for b in range(1, B):
                if b + 1 < B:
                    xn_low(b + 1)
                if b + 2 < B:
                    normalised(b + 2)
                if b == 1:
                    residual(XKVH * B - 1, B - 1)
                    statistics(B - 1)
                out_row(b)

        @block.tensor
        def _(pe):
            def project_keys_values(s, b, j):
                wait(pe, kT_lo, s)
                if not (isinstance(j, int) and j == 0):
                    pe.wait_ge(wkv_lo, j)
                rows = slice(b * S, (b + 1) * S)
                for t, src in enumerate((cT, xT)):
                    mm = split_matmuls(pe, ps_kv[:, t * NKV:(t + 1) * NKV],
                                       [(src[0][:, c, rows], src[1][:, c, rows], wkv[0][:, c, :], wkv[1][:, c, :])
                                        for c in range(C)])
                mm.then_inc(kv_ps, 1)

            def project_queries(s, b, j):
                wait(pe, qT_lo, s)
                if not (isinstance(j, int) and j == 0):
                    pe.wait_ge(wq_lo, j)
                rows = slice(b * S, (b + 1) * S)
                split_matmuls(pe, ps_q[:], [(xT[0][:, c, rows], xT[1][:, c, rows], wq[0][:, c, :], wq[1][:, c, :])
                                            for c in range(C)]).then_inc(q_ps, 1)

            def scores(s):
                pe.wait_ge(qT_lo, s + 1)
                pe.wait_ge(kT_lo, s + 1)
                wait(pe, exp_done, XG * s)
                for g in range(XG):
                    mm = split_matmuls(pe, ps_s[g // 2][:, g % 2 * KV:(g % 2 + 1) * KV],
                                       [(qT[0][:, g, :], qT[1][:, g, :], kT[0][:], kT[1][:])])
                    if g % 2:
                        mm.then_inc(s_ps, 1)

            def probs_transposed(s):
                pe.wait_ge(p_ok, 2 * s + 2)
                wait(pe, pT_lo, 2 * s)
                for t in range(2):
                    for g in range(XG):
                        mm = pe.transpose(ps_pT[t][:, g * S:(g + 1) * S], p[:, g, t * S:(t + 1) * S], ident[:])
                    mm.then_inc(pT_ps, 1)

            def queries_keys_transposed(s):
                pe.wait_ge(q_ok, s + 1)
                for g in range(XG):
                    mm = pe.transpose(ps_q[:, g * S:(g + 1) * S], q_sb[:, g, :], ident[:])
                mm.then_inc(qT_ps, 1)
                pe.wait_ge(v_lo, s + 1)
                pe.wait_ge(k_ok, s + 1)
                for t in range(2):
                    mm = pe.transpose(ps_kv[:, t * S:(t + 1) * S], k_sb[:, t, :], ident[:])
                mm.then_inc(kT_ps, 1)

            def project_output(s, j):
                pe.wait_ge(o_lo, s + 1)
                wait(pe, acc_ok, s)
                pe.wait_ge(wo_lo, j + 1)
                split_matmuls(pe, ps_y[:], [(oT[0][:, g, :], oT[1][:, g, :], wo[0][:, g, :], wo[1][:, g, :])
                                            for g in range(XG)]).then_inc(y_ps, 1)

            def values(s, b):
                pe.wait_ge(pT_lo, 2 * s + 2)
                split_matmuls(pe, ps_o[:], [(v[b % 2][0][:, t, :], v[b % 2][1][:, t, :],
                                             pT[0][:, t].rearrange("p g s -> p (g s)"), pT[1][:, t].rearrange("p g s -> p (g s)"))
                                            for t in range(2)]).then_inc(o_ps, 1)

            def xn_transposed(b):
                pe.wait_ge(xn_ok, b + 1)
                if b <= 1:
                    pe.wait_ge(kT_lo, XKVH * B)
                if b == 2:
                    pe.wait_ge(pT_lo, 2 * XKVH * B - 1)
                if b:
                    pe.wait_ge(xn_lo, max(b - 1, 1))
                for c in range(C):
                    start = 2 * P * (c % 2) + c // 2
                    mm = pe.transpose(ps_xn[b][:, c * S:(c + 1) * S], xn[:, b % 2, start:start + 2 * P - 1:2], ident[:])
                mm.then_inc(xnT_ps, 1)

            def linear(b):
                pe.wait_ge(xn_lo, b + 1)
                pe.wait_ge(w_lo, 2)
                if b == 0:
                    pe.wait_ge(qT_lo, XKVH * B)
                if b == 1:
                    pe.wait_ge(exp_done, XG * XKVH * B - 2)
                if b >= 2:
                    pe.wait_ge(out_ok, b - 1)
                x = xnT[b % 2]
                split_matmuls(pe, ps_f[b][:], [(x[0][:, c, :], x[1][:, c, :], w[0][:, c, :], w[1][:, c, :])
                                               for c in range(C)]).then_inc(f_ps, 1)

            queries_keys_transposed(0)

            def step(j, b, s, first, last):
                scores(s)
                if last:
                    xn_transposed(0)
                    project_output(s - 1, j)
                if not last:
                    following = j + 1 if b == B - 1 else j
                    project_keys_values(s + 1, (b + 1) % B, following)
                    project_queries(s + 1, (b + 1) % B, following)
                probs_transposed(s)
                if not last:
                    queries_keys_transposed(s + 1)
                    if not first:
                        project_output(s - 1, j - 1 if b == 0 else j)
                else:
                    xn_transposed(1)
                    linear(0)
                values(s, b)

            heads(pe, step)
            xn_transposed(2)
            linear(1)
            project_output(XKVH * B - 1, XKVH - 1)
            for b in range(2, B):
                if b + 1 < B:
                    xn_transposed(b + 1)
                linear(b)




def build(nc, io):
    with ExitStack() as ctx:
        def sb(name, shape, dt=F32):
            return ctx.enter_context(nc.sbuf_tensor(name, shape, dt))

        mem = {
            "x": sb("x", [P, B, D]),
            "xT": [sb(f"xT_{h}", [P, C, B * S], F32R) for h in ("hi", "lo")],
            "cT": [sb(f"cT_{h}", [P, C * B * S], F32R) for h in ("hi", "lo")],
            "ident": sb("ident", [P, P]),
            "minus_half": sb("minus_half", [P, 16]),
            "key_scale": sb("key_scale", [P, 1]),
            "raw_wq": sb("raw_wq", [P, C, D]),
            "raw_wkv": sb("raw_wkv", [P, C, 2 * XD]),
            "wq": [sb(f"wq_{h}", [P, C, D], F32R) for h in ("hi", "lo")],
            "wkv": [sb(f"wkv_{h}", [P, C, 2 * XD], F32R) for h in ("hi", "lo")],
            "ps_q": ctx.enter_context(nc.psum_tensor("ps_q", [P, 512], F32)),
            "ps_kv": ctx.enter_context(nc.psum_tensor("ps_kv", [P, 512], F32)),
            "q_ps": ctx.enter_context(nc.semaphore("b_q_ps")),
            "kv_ps": ctx.enter_context(nc.semaphore("b_kv_ps")),
        }
        self_attention(nc, mem, io)
        cross_attention_and_linear(nc, mem, io)


def kernel(**inputs):
    import numpy as np
    import concourse.bacc as bacc
    from concourse.bass_utils import run_bass_kernel_spmd as run

    a = {k: np.asarray(v) for k, v in inputs.items()}
    inv_freq = (1.0 / np.float32(10000.0) ** (np.arange(0, HD, 2, dtype=np.float32) / np.float32(HD))).astype(np.float32)
    angle = np.outer(np.arange(S, dtype=np.float32), inv_freq).astype(np.float32)
    cos, sin = np.cos(angle), np.sin(angle)
    cos, sin = np.concatenate([cos, cos], 1), np.concatenate([-sin, sin], 1)
    key_scale = np.float32(1 / np.sqrt(HD))
    laid = {
        "x": a["x"],
        "ctxT": a["ctx_4096"].reshape(B * S, C, P).transpose(1, 2, 0).reshape(C, P, 2, 512).transpose(0, 2, 1, 3).reshape(2 * C, P, 512),
        "a_wq": a["L0_attn_Wq"].T.reshape(C, P, D).transpose(1, 0, 2),
        "a_wkv": np.concatenate([a[w].T.reshape(C, P, KVH * HD) for w in ("L0_attn_Wk", "L0_attn_Wv")], 2).transpose(1, 0, 2),
        "a_wo": a["L0_attn_Wo"].T.reshape(KVH, G, HD, D).transpose(0, 2, 1, 3).reshape(P, G, D),
        "x_wq": a["L0_xattn_Wq"].reshape(C, P, XKVH, XG * XD).transpose(2, 1, 0, 3).reshape(XKVH, P, C * XG * XD),
        "x_wkv": np.concatenate([a[w].reshape(C, P, XKVH, XD).transpose(2, 1, 0, 3) for w in ("L0_xattn_Wk", "L0_xattn_Wv")],
                                3).reshape(XKVH, P, 2 * C * XD),
        "x_wo": a["L0_xattn_Wo"].reshape(XKVH, XG, XD, D).transpose(0, 2, 1, 3).reshape(XKVH, P, XG * D),
        "q4": a["L0_ffn_weight_q4"].reshape(D, 2 * P, 1).transpose(1, 2, 0).reshape(2, P, D),
        "q4_scale": a["L0_ffn_weight_scale"].reshape(D, D // 32).T,
        "bias": a["L0_ffn_bias"].reshape(1, D),
        "q_norm": a["L0_xattn_q_norm_w"].reshape(XD, 1),
        "k_norm": a["L0_xattn_k_norm_w"].reshape(XD, 1),
        "cos": np.stack([cos, cos * key_scale], 1).astype(np.float32),
        "sin": np.stack([sin, sin * key_scale], 1).astype(np.float32),
    }
    nc = bacc.Bacc("TRN2", target_bir_lowering=False, num_devices=1)
    arrays, io = {}, {}
    for name, array in laid.items():
        arrays["in_" + name] = np.ascontiguousarray(array)
        dt = mybir.dt.from_np(array.dtype)
        io[name] = nc.dram_tensor("in_" + name, array.shape, dt, kind="ExternalInput").ap()
    io["out"] = nc.dram_tensor("out_0", (B, S, D), F32, kind="ExternalOutput").ap()
    build(nc, io)
    return run(nc, [arrays], core_ids=[0]).results[0]["out_0"]
```
